# Optimizing a Trainium2 kernel written in Bass

```python
import numpy as np
import jax
import jax.numpy as jnp

def _softmax(x, axis=-1):
    return jax.nn.softmax(x, axis=axis)

def _gelu(x):
    return jax.nn.gelu(x, approximate=True)

def _silu(x):
    return jax.nn.silu(x)

def _sigmoid(x):
    return jax.nn.sigmoid(x)

def _layernorm(x, axis=-1, eps=1e-05):
    m = jnp.mean(x, axis=axis, keepdims=True)
    v = jnp.var(x, axis=axis, keepdims=True)
    return (x - m) / jnp.sqrt(v + eps)

def _scatter_add(tgt, idx, src, axis=0):
    return tgt.at[idx].add(src)

def _segment_sum(src, seg, n):
    return jax.ops.segment_sum(src, seg, n)
kernel_name = 'mk_prb_d1_jaxref_r4_65ac6d'

def setup_inputs(seed: int=0):
    np.random.seed(seed)
    _w = jnp.asarray

    def _L0_attn_setup():
        import jax, jax.numpy as jnp
        import numpy as np
        HEADS = 8
        DIM_HEAD = 64
        SCALE = DIM_HEAD ** (-0.5)
        key = jax.random.key(seed)
        k1, k2, k3 = jax.random.split(key, 3)
        B, N, D = (2, 512, 256)
        dim_inner = HEADS * DIM_HEAD
        x = jax.random.normal(k1, (B, N, D), dtype=jnp.float32)
        W_qkv = jax.random.normal(k2, (6 * dim_inner, D), dtype=jnp.float32) * 0.02
        W_out = jax.random.normal(k3, (D, dim_inner), dtype=jnp.float32) * 0.02
        return {'x': x, 'W_qkv': W_qkv, 'W_out': W_out}
    _L0_attn_in = _L0_attn_setup()

    def _L0_ffn_setup():
        import jax, jax.numpy as jnp
        import numpy as np
        DIM = 256
        HIDDEN = 768
        SCALE = 1.0 / 127.0

        def _dequant(w_int, dtype):
            return w_int.astype(dtype) * jnp.asarray(SCALE, dtype)
        key = jax.random.key(seed)
        k_x, k_g, k_u, k_d = jax.random.split(key, 4)
        x = jax.random.normal(k_x, (4, 512, DIM), dtype=jnp.float32)
        w_gate = jax.random.randint(k_g, (HIDDEN, DIM), -127, 128, dtype=jnp.int32)
        w_up = jax.random.randint(k_u, (HIDDEN, DIM), -127, 128, dtype=jnp.int32)
        w_down = jax.random.randint(k_d, (DIM, HIDDEN), -127, 128, dtype=jnp.int32)
        return {'x': x, 'w_gate': w_gate, 'w_up': w_up, 'w_down': w_down}
    _L0_ffn_in = _L0_ffn_setup()
    _d = {'L0_attn_x': _L0_attn_in['x'], 'L0_attn_W_qkv': _L0_attn_in['W_qkv'], 'L0_attn_W_out': _L0_attn_in['W_out'], 'L0_ffn_w_gate': _L0_ffn_in['w_gate'], 'L0_ffn_w_up': _L0_ffn_in['w_up'], 'L0_ffn_w_down': _L0_ffn_in['w_down']}
    _x0 = _d['L0_attn_x']
    _d['L0_attn_x'] = jax.random.normal(jax.random.fold_in(jax.random.key(seed), 1), (8, 512, 256), dtype=_x0.dtype)
    del _x0
    return _d

def reference(L0_attn_x, L0_attn_W_qkv, L0_attn_W_out, L0_ffn_w_gate, L0_ffn_w_up, L0_ffn_w_down):

    def _L0_attn_ref(x, W_qkv, W_out):
        import jax, jax.numpy as jnp
        import numpy as np
        HEADS = 8
        DIM_HEAD = 64
        SCALE = DIM_HEAD ** (-0.5)
        B, N, D = x.shape
        h, d = (HEADS, DIM_HEAD)
        qkvs = x @ W_qkv.T
        qkvs = qkvs.reshape(B, N, 6, h, d)
        qkvs = jnp.transpose(qkvs, (2, 0, 3, 1, 4))
        qu, ku, vu, qc, kc, vc = qkvs
        qu_s = qu * SCALE
        qc_s = qc * SCALE
        neg = -jnp.finfo(x.dtype).max
        causal_mask = jnp.triu(jnp.ones((N, N), dtype=bool), 1)
        term1 = jnp.einsum('bhid,bhjd->bhij', qc_s, vu)
        term1 = jnp.where(causal_mask, 0.0, term1)
        lookahead = jax.nn.sigmoid(jnp.einsum('bhid,bhjd->bhij', qu_s, ku))
        lookahead = jnp.where(causal_mask, lookahead, 0.0)
        Su = jnp.einsum('bhij,bhkj->bhik', term1, lookahead)
        Sc = jnp.einsum('bhid,bhjd->bhij', qc_s, kc)
        scores = Sc - jax.nn.silu(Su)
        scores = jnp.where(causal_mask, neg, scores)
        attn = jax.nn.softmax(scores, axis=-1)
        out = jnp.einsum('bhij,bhjd->bhid', attn, vc)
        out = jnp.transpose(out, (0, 2, 1, 3)).reshape(B, N, h * d)
        return out @ W_out.T

    def _L0_ffn_ref(x, w_gate, w_up, w_down):
        import jax, jax.numpy as jnp
        import numpy as np
        DIM = 256
        HIDDEN = 768
        SCALE = 1.0 / 127.0

        def _dequant(w_int, dtype):
            return w_int.astype(dtype) * jnp.asarray(SCALE, dtype)
        wg = _dequant(w_gate, x.dtype)
        wu = _dequant(w_up, x.dtype)
        wd = _dequant(w_down, x.dtype)
        gate = jnp.einsum('bsd,hd->bsh', x, wg)
        up = jnp.einsum('bsd,hd->bsh', x, wu)
        h = jax.nn.silu(gate) * up
        return jnp.einsum('bsh,dh->bsd', h, wd)
    x = L0_attn_x
    xn = _layernorm(x, axis=-1)
    x = x + _L0_attn_ref(xn, L0_attn_W_qkv, L0_attn_W_out) + _L0_ffn_ref(xn, L0_ffn_w_gate, L0_ffn_w_up, L0_ffn_w_down)
    return x

_drawn_inputs = setup_inputs


def setup_inputs(seed=0):
    import zlib

    import numpy as np

    out = dict(_drawn_inputs(seed))
    spreads = {}
    factors = {'L0_attn_W_qkv': 58.509, 'L0_attn_W_out': 57.19}
    for name, (base, spread) in spreads.items():
        noise = np.random.default_rng([zlib.crc32(name.encode()), seed]).standard_normal(out[name].shape)
        drawn = base * np.exp(spread * noise) if base else spread * noise
        out[name] = jnp.asarray(drawn.astype(out[name].dtype))
    for name, factor in factors.items():
        out[name] = (out[name] * factor).astype(out[name].dtype)
    return out
```

```python
import numpy as np
import concourse.bass as bass
from concourse import mybir
from contextlib import ExitStack

F32 = mybir.dt.float32
F32R = mybir.dt.float32r
BF16 = mybir.dt.bfloat16
I32 = mybir.dt.int32
ALU = mybir.AluOpType
ACT = mybir.ActivationFunctionType

P = 128
BATCH, SEQ, DIM = 8, 512, 256
HEADS, DH = 8, 64
INNER = HEADS * DH
HIDDEN = 768
KD = DIM // P
TT = SEQ // P
PAIRS = HEADS // 2
EPS = 1e-5
QU, KU, VU, QC, KC, VC = range(6)

TRI = 1280
GROUP = [(0, 512), (512, 512), (1024, 256)]
WIDE = {4: 0, 3: 512, 1: 896, 2: 1024}
ROWS = [(4,), (3, 1), (2,)]
HIGH, LOW = 0, 1
PRODUCTS = [(HIGH, HIGH), (HIGH, LOW), (LOW, HIGH)]

LOOK_SCALE = 1.0 / 16
SU_SCALE = 1.0 / 32
KC_FACTOR = -4.0
MASKED = 2.0 ** 100
NO_SCORE = 3.0e38


def split_weights(nc, W_qkv, W_high, W_low):
    tiles = 6 * INNER // P
    per = SEQ // P
    groups = 6 * KD
    ctx = ExitStack()
    with ctx:
        raw = ctx.enter_context(nc.sbuf_tensor("w_raw", [P, tiles, DIM], F32))
        ident = ctx.enter_context(nc.sbuf_tensor("w_ident", [P, P], F32))
        banks = [ctx.enter_context(nc.psum_tensor(f"w_bank{i}", [P, 512], F32)) for i in range(4)]
        loaded = [ctx.enter_context(nc.semaphore(f"w_loaded{i}")) for i in range(6)]
        zeroed = ctx.enter_context(nc.semaphore("w_zeroed"))
        ident_ready = ctx.enter_context(nc.semaphore("w_ident_ready"))
        turned = ctx.enter_context(nc.semaphore("w_turned"))
        high_done = ctx.enter_context(nc.semaphore("w_high_done"))
        low_done = ctx.enter_context(nc.semaphore("w_low_done"))
        block = ctx.enter_context(nc.Block())

        @block.sync
        def _(sp):
            for t in range(6):
                sp.dma_start(raw[:, per * t:per * (t + 1), :],
                             W_qkv[t * INNER:(t + 1) * INNER, :].rearrange("(n p) d -> p n d", p=P)) \
                  .then_inc(loaded[t], 16)

        @block.gpsimd
        def _(pool):
            pool.memset(ident[:, :], 0.0).then_inc(zeroed, 1)
            pool.wait_ge(zeroed, 1)
            pool.affine_select(out=ident[:, :], in_=ident[:, :], compare_op=ALU.not_equal, fill=1.0,
                               base=0, pattern=[[-1, P]], channel_multiplier=1).then_inc(ident_ready, 1)

        @block.tensor
        def _(pe):
            pe.wait_ge(ident_ready, 1)
            for n in range(groups):
                t, k = divmod(n, KD)
                if k == 0:
                    pe.wait_ge(loaded[t], 16)
                if n >= 4:
                    pe.wait_ge(low_done, n - 3)
                for i in range(per):
                    last = pe.transpose(banks[n % 4][:, i * P:(i + 1) * P],
                                        raw[:, per * t + i, k * P:(k + 1) * P], ident[:, :])
                last.then_inc(turned, 1)

        @block.scalar
        def _(act):
            for n in range(groups):
                t, k = divmod(n, KD)
                act.wait_ge(turned, n + 1)
                act.activation(W_high[:, k, t * INNER:(t + 1) * INNER], banks[n % 4][:, :], ACT.Copy,
                               scale=KC_FACTOR if t == KC else 1.0).then_inc(high_done, 1)

        @block.vector
        def _(dve):
            for n in range(groups):
                t, k = divmod(n, KD)
                dve.wait_ge(high_done, n + 1)
                dve.scalar_tensor_tensor(W_low[:, k, t * INNER:(t + 1) * INNER], banks[n % 4][:, :],
                                         KC_FACTOR if t == KC else 1.0,
                                         W_high[:, k, t * INNER:(t + 1) * INNER].bitcast(F32),
                                         ALU.mult, ALU.subtract).then_inc(low_done, 1)


X_BANKS = 3
PROJ_ORDER = [QC, KC, QU, KU, VU]
FIRST, MIDDLE, LAST = range(3)


def x_groups(s, part):
    out = []
    ahead = s < HEADS and (s < 6 or part != LAST)
    if s < HEADS:
        out += [("L", s, j) for j in range(3)]
    if s >= 2 or part != FIRST:
        out += [("PT", s, j) for j in range(3)]
    if ahead and s % 2 == 1:
        out += [("proj", s, QU)]
    if ahead and s == 6:
        out += [("XT", s, k) for k in range(KD)]
    if s < HEADS:
        out += [("T", s, j) for j in range(3)]
    if ahead:
        out += [("proj", s, t) for t in ((KU, VU) if s % 2 else (QC, KC))]
    if s < HEADS and s % 4 == 0:
        out += [("V", s, n) for n in range(2)]
    return out


def x_schedule():
    orders = []
    for part in (FIRST, MIDDLE, LAST):
        order = []
        if part == FIRST:
            order += [("XT", "first", k) for k in range(KD)]
            order += [("proj", -1, t) for t in PROJ_ORDER]
        for s in range(HEADS + (2 if part == LAST else 0)):
            order += x_groups(s, part)
        orders.append(order)
    shift = [(len(orders[MIDDLE]) - len(orders[FIRST])) % X_BANKS, 0, 0]
    held = {(n + len(orders[MIDDLE])) % X_BANKS: key for n, key in enumerate(orders[MIDDLE][-X_BANKS:], -X_BANKS)}
    parts = []
    for part, order in enumerate(orders):
        had, found = [0] * X_BANKS, {}
        before = {} if part == FIRST else {bank: (key, 1) for bank, key in held.items()}
        for n, key in enumerate(order):
            bank = (n + shift[part]) % X_BANKS
            had[bank] += 1
            found[key] = (bank, had[bank], before.get(bank))
            before[bank] = (key, 0)
        parts.append((found, had))
        if part < LAST:
            assert {bank: key for bank, (key, _) in before.items()} == held
    return parts


X_PLAN = x_schedule()


def attention(nc, x, W_high, W_low, heads_out):
    ctx = ExitStack()
    with ctx:
        def sb(name, shape, dt):
            return ctx.enter_context(nc.sbuf_tensor(name, shape, dt))

        def pb(name):
            return ctx.enter_context(nc.psum_tensor(name, [P, 512], F32))

        def sem(name):
            return ctx.enter_context(nc.semaphore(name))

        ident = sb("ident", [P, P], F32)
        ident16 = sb("ident16", [P, P], BF16)
        mask16 = sb("mask16", [P, P], BF16)
        xb = sb("xb", [P, TT, DIM], F32)
        stats = sb("stats", [P, TT, 6], F32)
        mean_var = sb("mean_var", [P, TT, 2], F32)
        var_eps = sb("var_eps", [P, TT], F32)
        minus_half = sb("minus_half", [P, TT], F32)
        rstd = sb("rstd", [P, TT], F32)
        xT = sb("xT", [P, 2, KD, SEQ], F32R)
        ku_s = sb("ku_s", [P, 2, SEQ], F32R)
        vu_s = sb("vu_s", [P, 2, SEQ], F32R)
        kc_s = sb("kc_s", [P, 2, 2, SEQ], F32R)
        qu_s = sb("qu_s", [P, 2, 2, SEQ], F32R)
        qc_s = sb("qc_s", [P, 2, 2, 2, SEQ], F32R)
        v_s = sb("v_s", [P, 2, 2, TT, 2 * P], F32R)
        tanh_l = sb("tanh_l", [P, TRI], F32)
        L_s = sb("L_s", [P, 2, 2, TRI], F32R)
        T_s = sb("T_s", [P, 2, 2, TRI], F32R)
        gate = sb("gate", [P, TRI], F32)
        prob = sb("prob", [P, 2, TRI], F32)
        least = sb("least", [P, 2, 4], F32)
        total = sb("total", [P, 2, 4], F32)
        inv = sb("inv", [P, 2, 4], F32)
        PT_s = sb("PT_s", [P, 2, TRI], F32R)
        o_s = sb("o_s", [P, 2, SEQ], F32)

        X = [pb(f"X{i}") for i in range(X_BANKS)]
        Su = [pb(f"Su{i}") for i in range(2)]
        Sc = [pb(f"Sc{i}") for i in range(2)]
        O = pb("O")

        x_filled = [sem(f"x_filled{i}") for i in range(X_BANKS)]
        consts = sem("consts")
        zeroed = sem("zeroed")
        x_loaded = sem("x_loaded")
        stats_done = sem("stats_done")
        agg_done = sem("agg_done")
        var_done = sem("var_done")
        rstd_done = sem("rstd_done")
        xn_done = sem("xn_done")
        xT_high = sem("xT_high")
        xT_low = sem("xT_low")
        proj_high = sem("proj_high")
        proj_low = sem("proj_low")
        q_low = sem("q_low")
        qc_twice = sem("qc_twice")
        qu_twice = sem("qu_twice")
        v_high = sem("v_high")
        v_low = sem("v_low")
        tanh_done = sem("tanh_done")
        tanh_masked = sem("tanh_masked")
        L_high = sem("L_high")
        L_ready = sem("L_ready")
        T_high = sem("T_high")
        T_low = sem("T_low")
        T_ready = sem("T_ready")
        scores_filled = sem("scores_filled")
        gate_done = sem("gate_done")
        silu_done = sem("silu_done")
        scores_emptied = sem("scores_emptied")
        exp_done = sem("exp_done")
        inv_done = sem("inv_done")
        prob_ready = sem("prob_ready")
        PT_high = sem("PT_high")
        PT_low = sem("PT_low")
        o_filled = sem("o_filled")
        o_copied = sem("o_copied")
        o_stored = [sem(f"o_stored{i}") for i in range(2)]
        ticks = sem("ticks")

        def x_use(part, b, key):
            found, had = X_PLAN[part]
            bank, nth, _ = found[key]
            if part == FIRST:
                return bank, nth
            n0, n1 = X_PLAN[FIRST][1][bank], X_PLAN[MIDDLE][1][bank]
            return bank, (b - 1) * n1 + n0 + nth if part == MIDDLE else (BATCH - 2) * n1 + n0 + nth

        def wait_before(eng, signal, value):
            eng.wait_ge(signal, value)
            eng.sem_inc(ticks, 1)

        def after(n, per, j):
            return n * per + j + 1

        def proj_count(q, t):
            return q * 5 + PROJ_ORDER.index(t) + 1

        def x_read(b, key):
            kind, s, n = key
            if kind == "XT":
                return xT_low, after(0 if s == "first" else b + 1, KD, n)
            if kind == "L":
                return tanh_done, after(b * HEADS + s, 3, n)
            if kind == "T":
                return T_low, after(b * HEADS + s, 3, n)
            if kind == "PT":
                return PT_low, after(b * HEADS + s - 2, 3, n)
            if kind == "V":
                return v_low, after(b, 4, 2 * (s // 4) + n)
            return proj_low, proj_count(b * PAIRS + (0 if s < 0 else s // 2 + 1), n)

        block = ctx.enter_context(nc.Block())

        def batches(eng, program):
            program(0, FIRST)
            with eng.Fori(1, BATCH - 1) as b:
                program(b, MIDDLE)
            program(BATCH - 1, LAST)

        def steps(part):
            return range(HEADS + (2 if part == LAST else 0))

        @block.sync
        def _(sp):
            def load_x(b):
                sp.dma_start(xb[:, :, :], x[bass.ds(b * SEQ, SEQ), :].rearrange("(n p) d -> p n d", p=P)) \
                  .then_inc(x_loaded, 16)

            def program(b, part):
                for s in steps(part):
                    g = b * HEADS + s
                    if s == 0 and part != LAST:
                        sp.wait_ge(xT_low, b * KD + KD)
                        sp.sem_inc(ticks, 1)
                        load_x(b + 1)
                    if s < HEADS and (s < 6 or part != LAST):
                        q = b * PAIRS + s // 2 + 1
                        if s % 2 == 0:
                            dup(QC, q, (s // 2 + 1) % 2)
                        else:
                            dup(QU, q, 0)
                    if s >= 2 or part != FIRST:
                        if s % 2 == 1:
                            par = ((s - 3) // 2) % 2
                            sp.wait_ge(o_copied, g - 1)
                            sp.sem_inc(ticks, 1)
                            sp.dma_start(heads_out[bass.ds((b * PAIRS + (s - 3) // 2) * P, P), :],
                                         o_s[:, par, :]).then_inc(o_stored[par], 16)
                if part == LAST:
                    sp.wait_ge(o_stored[0], 16 * BATCH * PAIRS // 2)
                    sp.wait_ge(o_stored[1], 16 * BATCH * PAIRS // 2)

            def dup(t, q, par):
                sp.wait_ge(proj_low, proj_count(q, t))
                sp.sem_inc(ticks, 1)
                tile, done = (qc_s[:, par], qc_twice) if t == QC else (qu_s[:, :], qu_twice)
                words = tile.bitcast(F32)
                sp.dma_start(words[DH:P, 0, :, :], words[0:DH, 0, :, :]).then_inc(done, 16)
                sp.dma_start(words[0:DH, 1, :, :], words[DH:P, 1, :, :]).then_inc(done, 16)

            load_x(0)
            dup(QC, 0, 0)
            dup(QU, 0, 0)
            batches(sp, program)

        @block.gpsimd
        def _(pool):
            pool.memset(ident[:, :], 0.0).then_inc(zeroed, 1)
            pool.memset(ident16[:, :], 0.0).then_inc(zeroed, 1)
            pool.memset(mask16[:, :], 0.0).then_inc(zeroed, 1)
            pool.memset(minus_half[:, :], -0.5).then_inc(consts, 1)
            pool.wait_ge(zeroed, 3)
            for m in (ident, ident16):
                pool.affine_select(out=m[:, :], in_=m[:, :], compare_op=ALU.not_equal, fill=1.0,
                                   base=0, pattern=[[-1, P]], channel_multiplier=1).then_inc(consts, 1)
            pool.affine_select(out=mask16[:, :], in_=mask16[:, :], compare_op=ALU.is_ge, fill=MASKED,
                               base=0, pattern=[[-1, P]], channel_multiplier=1).then_inc(consts, 1)
            pool.wait_ge(consts, 4)

            def rstd_of(b):
                pool.wait_ge(var_done, b + 1)
                pool.tensor_tensor(rstd[:, :], var_eps[:, :], minus_half[:, :], ALU.pow).then_inc(rstd_done, 1)

            def mask_tanh(g, j):
                wait_before(pool, tanh_done, after(g, 3, j))
                first, n = [(WIDE[4] + 384, 1), (WIDE[3] + 256, 2), (WIDE[2] + 128, 1)][j]
                v = tanh_l[:, first:first + n * P].rearrange("p (n c) -> p n c", n=n)
                pool.affine_select(out=v, in_=v, compare_op=ALU.is_ge, fill=-1.0, base=-1,
                                   pattern=[[0, n], [-1, P]], channel_multiplier=1).then_inc(tanh_masked, 1)

            def mask_T(g, par, j):
                wait_before(pool, T_low, after(g, 3, j))
                for i, w in enumerate(ROWS[j]):
                    v = T_s[:, par, :, WIDE[w]:WIDE[w] + P]
                    last = pool.affine_select(out=v, in_=v.bitcast(F32), compare_op=ALU.is_ge, fill=0.0,
                                              base=0, pattern=[[0, 2], [1, P]], channel_multiplier=-1)
                last.then_inc(T_ready, 1)

            def norm(g, s, j):
                hp = s % 2
                wait_before(pool, inv_done, after(g, 3, j))
                for w in ROWS[j]:
                    v = prob[:, hp, WIDE[w]:WIDE[w] + w * P]
                    last = pool.tensor_scalar(v, v, inv[:, hp, w - 1:w], None, ALU.mult)
                last.then_inc(prob_ready, 1)

            def program(b, part):
                for s in steps(part)[0:HEADS + 1]:
                    g = b * HEADS + s
                    back1 = s >= 1 or part != FIRST
                    if s < HEADS:
                        for j in range(3):
                            mask_tanh(g, j)
                    if back1:
                        norm(g - 1, (s - 1) % HEADS, 0)
                    if s < HEADS:
                        for j in range(3):
                            mask_T(g, s % 2, j)
                    if back1:
                        norm(g - 1, (s - 1) % HEADS, 1)
                        norm(g - 1, (s - 1) % HEADS, 2)
                    if s == 4 and part != LAST:
                        rstd_of(b + 1)

            rstd_of(0)
            batches(pool, program)

        @block.tensor
        def _(pe):
            def into_x(part, b, key):
                bank, _ = x_use(part, b, key)
                before = X_PLAN[part][0][key][2]
                if before:
                    pe.wait_ge(*x_read(b - before[1], before[0]))
                return X[bank], x_filled[bank]

            def transpose_x(part, b, s, nb):
                pe.wait_ge(xn_done, nb + 1)
                for k in range(KD):
                    bank, filled = into_x(part, b, ("XT", s, k))
                    for n in range(TT):
                        last = pe.transpose(bank[:, n * P:(n + 1) * P], xb[:, n, k * P:(k + 1) * P], ident[:, :])
                    last.then_inc(filled, 1)

            def project(part, b, s, t, p):
                bank, filled = into_x(part, b, ("proj", s, t))
                cols = slice(t * INNER + p * P, t * INNER + (p + 1) * P)
                n = 0
                for k in range(KD):
                    for a, c in PRODUCTS:
                        W = (W_high, W_low)[a]
                        last = pe.matmul(bank[:, :], W[:, k, cols], xT[:, c, k, :],
                                         start=(n == 0), stop=(n == 3 * KD - 1))
                        n += 1
                last.then_inc(filled, 1)

            def values(part, b, s, n):
                bank, filled = into_x(part, b, ("V", s, n))
                cols = slice(VC * INNER + (s // 4) * 2 * P, VC * INNER + (s // 4 + 1) * 2 * P)
                for i in range(2):
                    tok = slice((2 * n + i) * P, (2 * n + i + 1) * P)
                    m = 0
                    for k in range(KD):
                        for a, c in PRODUCTS:
                            W = (W_high, W_low)[c]
                            last = pe.matmul(bank[:, i * 256:(i + 1) * 256], xT[:, a, k, tok], W[:, k, cols],
                                             start=(m == 0), stop=(m == 3 * KD - 1))
                            m += 1
                last.then_inc(filled, 1)

            def look_ahead(part, b, s):
                for j in range(3):
                    bank, filled = into_x(part, b, ("L", s, j))
                    for w in ROWS[j]:
                        J, at = w - 1, WIDE[w] - GROUP[j][0]
                        for a in (HIGH, LOW):
                            last = pe.matmul(bank[:, at:at + w * P], ku_s[:, s % 2, J * P:(J + 1) * P],
                                             qu_s[:, s % 2, a, 0:w * P], start=(a == 0), stop=(a == 1))
                    last.then_inc(filled, 1)

            def term1(part, b, s):
                par = (s // 2) % 2
                for j in range(3):
                    bank, filled = into_x(part, b, ("T", s, j))
                    for w in ROWS[j]:
                        J, at = TT - w, WIDE[w] - GROUP[j][0]
                        for a in (HIGH, LOW):
                            last = pe.matmul(bank[:, at:at + w * P], vu_s[:, s % 2, J * P:(J + 1) * P],
                                             qc_s[:, par, s % 2, a, J * P:SEQ], start=(a == 0), stop=(a == 1))
                    last.then_inc(filled, 1)

            def scores(g, s, j):
                hp, par, slot = s % 2, (s // 2) % 2, (s + j) % 2
                if not (isinstance(g, int) and 3 * g + j < 2):
                    pe.wait_ge(scores_emptied, 3 * g + j - 1)
                for w in ROWS[j]:
                    I, at = w - 1, WIDE[w] - GROUP[j][0]
                    for a in (HIGH, LOW):
                        pe.matmul(Sc[slot][:, at:at + w * P], qc_s[:, par, hp, a, I * P:(I + 1) * P],
                                  kc_s[:, par, hp, 0:w * P], start=(a == 0), stop=False)
                    pe.matmul(Sc[slot][:, at + I * P:at + w * P], ident16[:, :], mask16[:, :],
                              start=False, stop=True)
                if j == 0:
                    pe.wait_ge(T_ready, after(g, 3, 2))
                    pe.wait_ge(L_ready, after(g, 3, 2))
                for w in ROWS[j]:
                    I, at = w - 1, WIDE[w] - GROUP[j][0]
                    for J in range(I, -1, -1):
                        to = WIDE[TT - J] + (I - J) * P
                        for n, (a, c) in enumerate(PRODUCTS):
                            last = pe.matmul(Su[slot][:, at:at + (J + 1) * P], T_s[:, hp, a, to:to + P],
                                             L_s[:, hp, c, WIDE[J + 1]:WIDE[J + 1] + (J + 1) * P],
                                             start=(J == I and n == 0), stop=(J == 0 and n == 2))
                last.then_inc(scores_filled, 1)

            def turn_probs(part, b, s, g):
                hp = s % 2
                pe.wait_ge(prob_ready, after(g, 3, 2))
                for j in range(3):
                    bank, filled = into_x(part, b, ("PT", s, j))
                    for w in ROWS[j]:
                        K, at = TT - w, WIDE[w] - GROUP[j][0]
                        for I in range(K, TT):
                            last = pe.transpose(bank[:, at + (I - K) * P:at + (I - K + 1) * P],
                                                prob[:, hp, WIDE[I + 1] + K * P:WIDE[I + 1] + (K + 1) * P],
                                                ident[:, :])
                    last.then_inc(filled, 1)

            def attend(s, g):
                slot = (s - 2) % HEADS
                if not (isinstance(g, int) and g == 0):
                    pe.wait_ge(o_copied, g)
                pe.wait_ge(PT_low, after(g, 3, 2))
                cols = slice((slot // 2 % 2) * P, (slot // 2 % 2 + 1) * P)
                for K in range(TT):
                    at = WIDE[TT - K]
                    for n, (a, c) in enumerate(PRODUCTS):
                        last = pe.matmul(O[:, K * P:SEQ], v_s[:, slot // 4, a, K, cols],
                                         PT_s[:, c, at:at + (TT - K) * P],
                                         start=(K == 0 and n == 0), stop=(K == TT - 1 and n == 2))
                last.then_inc(o_filled, 1)

            def program(b, part):
                for s in steps(part):
                    g = b * HEADS + s
                    back1 = (s >= 1 or part != FIRST) and s <= HEADS
                    back2 = s >= 2 or part != FIRST
                    q = b * PAIRS + s // 2
                    ahead = s < HEADS and (s < 6 or part != LAST)
                    if back1:
                        scores(g - 1, (s - 1) % HEADS, 0)
                    if s < HEADS:
                        if s % 2 == 0:
                            pe.wait_ge(proj_low, proj_count(q, VU))
                            pe.wait_ge(qu_twice, (q + 1) * 32)
                            pe.wait_ge(qc_twice, (q + 1) * 32)
                        look_ahead(part, b, s)
                    if back2:
                        turn_probs(part, b, s, g - 2)
                    if back1:
                        scores(g - 1, (s - 1) % HEADS, 1)
                    if s % 2 == 1 and ahead:
                        project(part, b, s, QU, (s // 2 + 1) % PAIRS)
                    if s == 6 and ahead:
                        transpose_x(part, b, s, b + 1)
                    if back2:
                        if (s - 2) % 4 == 0:
                            pe.wait_ge(v_low, 4 * b + 2 * ((s - 2) // 4) + 2)
                        attend(s, g - 2)
                    if s < HEADS:
                        term1(part, b, s)
                    if back1:
                        scores(g - 1, (s - 1) % HEADS, 2)
                    if ahead:
                        if s == 6:
                            pe.wait_ge(xT_low, (b + 1) * KD + KD)
                        for t in ((KU, VU) if s % 2 else (QC, KC)):
                            project(part, b, s, t, (s // 2 + 1) % PAIRS)
                    if s < HEADS and s % 4 == 0:
                        for n in range(2):
                            values(part, b, s, n)

            pe.wait_ge(consts, 4)
            transpose_x(FIRST, 0, "first", 0)
            pe.wait_ge(xT_low, KD)
            for t in PROJ_ORDER:
                project(FIRST, 0, -1, t, 0)
            batches(pe, program)

        @block.scalar
        def _(act):
            def from_x(part, b, key):
                bank, nth = x_use(part, b, key)
                act.wait_ge(x_filled[bank], nth)
                return X[bank]

            def high_xT(part, b, s):
                for k in range(KD):
                    bank = from_x(part, b, ("XT", s, k))
                    act.activation(xT[:, HIGH, k, :], bank[:, :], ACT.Copy).then_inc(xT_high, 1)

            def high_proj(part, b, s, t, par):
                bank = from_x(part, b, ("proj", s, t))
                for h in range(2):
                    rows = slice(h * DH, (h + 1) * DH)
                    dst = {KU: ku_s[rows, h, :], VU: vu_s[rows, h, :], KC: kc_s[rows, par, h, :],
                           QU: qu_s[rows, h, HIGH, :], QC: qc_s[rows, par, h, HIGH, :]}[t]
                    last = act.activation(dst, bank[rows, :], ACT.Copy)
                last.then_inc(proj_high, 1)

            def high_values(part, b, s, n):
                bank = from_x(part, b, ("V", s, n))
                act.activation(v_s[:, s // 4, HIGH, 2 * n:2 * n + 2, :], bank[:, :].rearrange("p (n c) -> p n c", n=2),
                               ACT.Copy).then_inc(v_high, 1)

            def tanh_of_L(part, b, s, g, j):
                bank = from_x(part, b, ("L", s, j))
                c, n = GROUP[j]
                if not (isinstance(g, int) and g == 0):
                    act.wait_ge(L_ready, after(g - 1, 3, j))
                act.activation(tanh_l[:, c:c + n], bank[:, 0:n], ACT.Tanh, scale=LOOK_SCALE).then_inc(tanh_done, 1)

            def high_T(part, b, s, g, j):
                bank = from_x(part, b, ("T", s, j))
                c, n = GROUP[j]
                if not (isinstance(g, int) and g < 2):
                    act.wait_ge(scores_filled, after(g - 2, 3, 2))
                act.activation(T_s[:, s % 2, HIGH, c:c + n], bank[:, 0:n], ACT.Copy).then_inc(T_high, 1)

            def high_L(g, s, j):
                c, n = GROUP[j]
                act.wait_ge(tanh_masked, after(g, 3, j))
                if not (isinstance(g, int) and g < 2):
                    act.wait_ge(scores_filled, after(g - 2, 3, 2))
                act.activation(L_s[:, s % 2, HIGH, c:c + n], tanh_l[:, c:c + n], ACT.Copy, bias=1.0) \
                   .then_inc(L_high, 1)

            def gate_of(g, s, j):
                c, n = GROUP[j]
                if not (isinstance(g, int) and g == 0):
                    act.wait_ge(scores_emptied, after(g - 1, 3, j))
                act.wait_ge(scores_filled, after(g, 3, j))
                act.activation(gate[:, c:c + n], Su[(s + j) % 2][:, 0:n], ACT.Tanh, scale=SU_SCALE) \
                   .then_inc(gate_done, 1)

            def exp_of(g, s, j):
                hp = s % 2
                act.wait_ge(scores_emptied, after(g, 3, j))
                for w in ROWS[j]:
                    v = prob[:, hp, WIDE[w]:WIDE[w] + w * P]
                    last = act.activation(v, v, ACT.Exp, bias=least[:, hp, w - 1:w], scale=-1.0,
                                          accum_out=total[:, hp, w - 1:w])
                last.then_inc(exp_done, 1)

            def high_PT(part, b, s, g, j):
                bank = from_x(part, b, ("PT", s, j))
                c, n = GROUP[j]
                if not (isinstance(g, int) and g == 0):
                    act.wait_ge(o_filled, g)
                act.activation(PT_s[:, HIGH, c:c + n], bank[:, 0:n], ACT.Copy).then_inc(PT_high, 1)

            def copy_o(b, s, g):
                slot = (s - 2) % HEADS
                rows, par = slice((slot % 2) * DH, (slot % 2 + 1) * DH), (slot // 2) % 2
                act.wait_ge(o_filled, g + 1)
                if slot % 2 == 0 and not (isinstance(b, int) and b * PAIRS + (s - 2) // 2 < 2):
                    act.wait_ge(o_stored[par], ((b * PAIRS + (s - 2) // 2 - par) // 2) * 16
                                if isinstance(b, int) else (b * (PAIRS // 2) + ((s - 2) // 2 - par) // 2) * 16)
                act.activation(o_s[rows, par, :], O[rows, :], ACT.Copy).then_inc(o_copied, 1)

            def program(b, part):
                for s in steps(part):
                    g = b * HEADS + s
                    back1 = (s >= 1 or part != FIRST) and s <= HEADS
                    back2 = s >= 2 or part != FIRST
                    ahead = s < HEADS and (s < 6 or part != LAST)
                    par = (s // 2 + 1) % 2
                    s1 = (s - 1) % HEADS
                    if back1:
                        gate_of(g - 1, s1, 0)
                    if s < HEADS:
                        for j in range(3):
                            tanh_of_L(part, b, s, g, j)
                    if back1:
                        exp_of(g - 1, s1, 0)
                    for j in range(3):
                        if back2:
                            high_PT(part, b, s, g - 2, j)
                        if s < HEADS:
                            high_L(g, s, j)
                    if back1:
                        gate_of(g - 1, s1, 1)
                    if s % 2 == 1 and ahead:
                        high_proj(part, b, s, QU, par)
                    if s == 6 and ahead:
                        high_xT(part, b, s)
                    if s < HEADS:
                        for j in range(3):
                            high_T(part, b, s, g, j)
                    if back1:
                        exp_of(g - 1, s1, 1)
                        gate_of(g - 1, s1, 2)
                    if back2:
                        copy_o(b, s, g - 2)
                    if ahead:
                        for t in ((KU, VU) if s % 2 else (QC, KC)):
                            high_proj(part, b, s, t, par)
                    if back1:
                        exp_of(g - 1, s1, 2)
                    if s < HEADS and s % 4 == 0:
                        for n in range(2):
                            high_values(part, b, s, n)

            high_xT(FIRST, 0, "first")
            for t in PROJ_ORDER:
                high_proj(FIRST, 0, -1, t, 0)
            batches(act, program)

        @block.vector
        def _(dve):
            def x_bank(part, key):
                return X[X_PLAN[part][0][key][0]]

            def low_xT(part, b, s, nb):
                for k in range(KD):
                    bank = x_bank(part, ("XT", s, k))
                    dve.wait_ge(xT_high, nb * KD + k + 1)
                    dve.tensor_tensor(xT[:, LOW, k, :], bank[:, :], xT[:, HIGH, k, :].bitcast(F32), ALU.subtract) \
                       .then_inc(xT_low, 1)

            def low_proj(part, b, s, t, par, q):
                bank = x_bank(part, ("proj", s, t))
                dve.wait_ge(proj_high, proj_count(q, t))
                for h in range(2):
                    rows, other = slice(h * DH, (h + 1) * DH), slice((1 - h) * DH, (2 - h) * DH)
                    high, out = {KU: (ku_s[rows, h, :], ku_s[other, h, :]),
                                 VU: (vu_s[rows, h, :], vu_s[other, h, :]),
                                 KC: (kc_s[rows, par, h, :], kc_s[other, par, h, :]),
                                 QU: (qu_s[rows, h, HIGH, :], qu_s[rows, h, LOW, :]),
                                 QC: (qc_s[rows, par, h, HIGH, :], qc_s[rows, par, h, LOW, :])}[t]
                    last = dve.tensor_tensor(out, bank[rows, :], high.bitcast(F32), ALU.subtract)
                last.then_inc(proj_low, 1)

            def low_values(part, b, s, n):
                bank = x_bank(part, ("V", s, n))
                dve.wait_ge(v_high, 4 * b + 2 * (s // 4) + n + 1)
                dve.tensor_tensor(v_s[:, s // 4, LOW, 2 * n:2 * n + 2, :],
                                  bank[:, :].rearrange("p (n c) -> p n c", n=2),
                                  v_s[:, s // 4, HIGH, 2 * n:2 * n + 2, :].bitcast(F32), ALU.subtract) \
                   .then_inc(v_low, 1)

            def low_L(g, s, j):
                c, n = GROUP[j]
                dve.wait_ge(L_high, after(g, 3, j))
                dve.scalar_tensor_tensor(L_s[:, s % 2, LOW, c:c + n], tanh_l[:, c:c + n], 1.0,
                                         L_s[:, s % 2, HIGH, c:c + n].bitcast(F32), ALU.add, ALU.subtract) \
                   .then_inc(L_ready, 1)

            def low_T(part, b, s, g, j):
                bank = x_bank(part, ("T", s, j))
                c, n = GROUP[j]
                dve.wait_ge(T_high, after(g, 3, j))
                dve.tensor_tensor(T_s[:, s % 2, LOW, c:c + n], bank[:, 0:n],
                                  T_s[:, s % 2, HIGH, c:c + n].bitcast(F32), ALU.subtract) \
                   .then_inc(T_low, 1)

            def silu_of(g, s, j):
                c, n = GROUP[j]
                dve.wait_ge(gate_done, after(g, 3, j))
                dve.scalar_tensor_tensor(gate[:, c:c + n], gate[:, c:c + n], 1.0, Su[(s + j) % 2][:, 0:n],
                                         ALU.add, ALU.mult).then_inc(silu_done, 1)

            def minus_scores(g, s, j):
                hp = s % 2
                wait_before(dve, silu_done, after(g, 3, j))
                if j == 0 and not (isinstance(g, int) and g < 2):
                    wait_before(dve, PT_high, after(g - 2, 3, 2))
                for w in ROWS[j]:
                    at = WIDE[w] - GROUP[j][0]
                    last = dve.tensor_tensor_reduce(prob[:, hp, WIDE[w]:WIDE[w] + w * P],
                                                    Sc[(s + j) % 2][:, at:at + w * P],
                                                    gate[:, WIDE[w]:WIDE[w] + w * P], SU_SCALE, NO_SCORE,
                                                    ALU.add, ALU.min, least[:, hp, w - 1:w])
                last.then_inc(scores_emptied, 1)

            def inverse(g, s, j):
                hp = s % 2
                for i, w in enumerate(ROWS[j]):
                    if i == 0:
                        dve.wait_ge(exp_done, after(g, 3, j))
                    last = dve.reciprocal(inv[:, hp, w - 1:w], total[:, hp, w - 1:w])
                last.then_inc(inv_done, 1)

            def low_PT(part, b, s, g, j):
                bank = x_bank(part, ("PT", s, j))
                c, n = GROUP[j]
                dve.wait_ge(PT_high, after(g, 3, j))
                dve.tensor_tensor(PT_s[:, LOW, c:c + n], bank[:, 0:n],
                                  PT_s[:, HIGH, c:c + n].bitcast(F32), ALU.subtract) \
                   .then_inc(PT_low, 1)

            def x_stats(nb):
                for n in range(TT):
                    if n == 0:
                        dve.wait_ge(x_loaded, (nb + 1) * 16)
                    last = dve.bn_stats(stats[:, n, :], xb[:, n, :])
                last.then_inc(stats_done, 1)
                wait_before(dve, stats_done, nb + 1)
                for n in range(TT):
                    last = dve.bn_aggr(mean_var[:, n, :], stats[:, n, :])
                last.then_inc(agg_done, 1)
                dve.wait_ge(agg_done, nb + 1)
                dve.tensor_scalar(var_eps[:, :], mean_var[:, :, 1], EPS, None, ALU.add).then_inc(var_done, 1)

            def x_norm(nb):
                for n in range(TT):
                    if n == 0:
                        dve.wait_ge(rstd_done, nb + 1)
                    last = dve.tensor_scalar(xb[:, n, :], xb[:, n, :], mean_var[:, n, 0:1], rstd[:, n:n + 1],
                                             ALU.subtract, ALU.mult)
                last.then_inc(xn_done, 1)

            def program(b, part):
                for s in steps(part):
                    g = b * HEADS + s
                    back1 = (s >= 1 or part != FIRST) and s <= HEADS
                    back2 = s >= 2 or part != FIRST
                    ahead = s < HEADS and (s < 6 or part != LAST)
                    par, q = (s // 2 + 1) % 2, b * PAIRS + s // 2 + 1
                    s1 = (s - 1) % HEADS
                    if back1:
                        silu_of(g - 1, s1, 0)
                        minus_scores(g - 1, s1, 0)
                    for j in range(3):
                        if back2:
                            low_PT(part, b, s, g - 2, j)
                        if s < HEADS:
                            low_L(g, s, j)
                    if back1:
                        silu_of(g - 1, s1, 1)
                        inverse(g - 1, s1, 0)
                        minus_scores(g - 1, s1, 1)
                    if s % 2 == 1 and ahead:
                        low_proj(part, b, s, QU, par, q)
                    if s == 6 and ahead:
                        low_xT(part, b, s, b + 1)
                    if s < HEADS:
                        low_T(part, b, s, g, 0)
                        low_T(part, b, s, g, 1)
                    if back1:
                        silu_of(g - 1, s1, 2)
                    if s < HEADS:
                        low_T(part, b, s, g, 2)
                    if back1:
                        minus_scores(g - 1, s1, 2)
                        inverse(g - 1, s1, 1)
                    if ahead:
                        for t in ((KU, VU) if s % 2 else (QC, KC)):
                            low_proj(part, b, s, t, par, q)
                    if back1:
                        inverse(g - 1, s1, 2)
                    if s < HEADS and s % 4 == 0:
                        for n in range(2):
                            low_values(part, b, s, n)
                    if s == 3 and part != LAST:
                        x_stats(b + 1)
                    if s == 5 and part != LAST:
                        x_norm(b + 1)

            x_stats(0)
            x_norm(0)
            low_xT(FIRST, 0, "first", 0)
            for t in PROJ_ORDER:
                low_proj(FIRST, 0, -1, t, 0, 0)
            batches(dve, program)


def ffn_and_sum(nc, x, w_gate, w_up, w_down, W_out, heads_out, out):
    HT = HIDDEN // P
    OT = INNER // P
    ctx = ExitStack()
    with ctx:
        def sb(name, shape, dt):
            return ctx.enter_context(nc.sbuf_tensor(name, shape, dt))

        def sem(name):
            return ctx.enter_context(nc.semaphore(name))

        raw_gate = sb("f_raw_gate", [P, HT, DIM], I32)
        raw_up = sb("f_raw_up", [P, HT, DIM], I32)
        raw_down = sb("f_raw_down", [P, KD, HIDDEN], I32)
        nat_gate = sb("f_nat_gate", [P, HT, DIM], F32)
        nat_up = sb("f_nat_up", [P, HT, DIM], F32)
        nat_down = sb("f_nat_down", [P, KD, HIDDEN], F32)
        nat_out = sb("f_nat_out", [P, KD, INNER], F32)
        gate_w = sb("f_gate_w", [P, 2, KD, HIDDEN], F32R)
        up_w = sb("f_up_w", [P, 2, KD, HIDDEN], F32R)
        down_w = sb("f_down_w", [P, 2, HT, DIM], F32R)
        out_w = sb("f_out_w", [P, 2, OT, DIM], F32R)
        ident = sb("f_ident", [P, P], F32)
        xb = sb("f_xb", [P, TT, DIM], F32)
        xres = sb("f_xres", [P, TT, DIM], F32)
        stats = sb("f_stats", [P, TT, 6], F32)
        mean_var = sb("f_mean_var", [P, TT, 2], F32)
        var_eps = sb("f_var_eps", [P, TT], F32)
        minus_half = sb("f_minus_half", [P, TT], F32)
        rstd = sb("f_rstd", [P, TT], F32)
        xT = sb("f_xT", [P, 2, KD, SEQ], F32R)
        act_s = sb("f_act", [P, 2, SEQ], F32)
        h_s = sb("f_h", [P, 2, HT, SEQ], F32R)
        o_in = sb("f_o_in", [P, OT, SEQ], F32)
        o_s = sb("f_o", [P, 2, OT, SEQ], F32R)
        y_s = sb("f_y", [P, TT, DIM], F32)

        def pb(name):
            return ctx.enter_context(nc.psum_tensor(name, [P, 512], F32))

        G = [pb(f"f_G{i}") for i in range(2)]
        U = [pb(f"f_U{i}") for i in range(2)]
        Y = [pb(f"f_Y{i}") for i in range(2)]
        XT = [pb(f"f_XT{i}") for i in range(2)]

        w_loaded = [sem(f"f_w_loaded{i}") for i in range(4)]
        zeroed = sem("f_zeroed")
        consts = sem("f_consts")
        dequantized = sem("f_dequantized")
        w_turned = sem("f_w_turned")
        w_high = sem("f_w_high")
        w_low = sem("f_w_low")
        x_loaded = sem("f_x_loaded")
        xres_loaded = sem("f_xres_loaded")
        o_loaded = sem("f_o_loaded")
        stats_done = sem("f_stats_done")
        agg_done = sem("f_agg_done")
        var_done = sem("f_var_done")
        rstd_done = sem("f_rstd_done")
        xn_done = sem("f_xn_done")
        xT_filled = sem("f_xT_filled")
        xT_high = sem("f_xT_high")
        xT_low = sem("f_xT_low")
        gu_filled = sem("f_gu_filled")
        tanh_done = sem("f_tanh_done")
        gated = sem("f_gated")
        hidden_done = sem("f_hidden_done")
        h_high = sem("f_h_high")
        h_low = sem("f_h_low")
        o_high = sem("f_o_high")
        o_low = sem("f_o_low")
        y_filled = sem("f_y_filled")
        y_done = sem("f_y_done")
        y_stored = sem("f_y_stored")
        ticks = sem("f_ticks")

        def wait_before(eng, signal, value):
            eng.wait_ge(signal, value)
            eng.sem_inc(ticks, 1)

        weight_groups = []
        for which, nat, w in ((0, nat_gate, gate_w), (1, nat_up, up_w)):
            for k in range(KD):
                for a, b in ((0, 4), (4, HT)):
                    weight_groups.append((which, [nat[:, m, k * P:(k + 1) * P] for m in range(a, b)],
                                          w[:, HIGH, k, a * P:b * P], w[:, LOW, k, a * P:b * P], 1.0))
        for which, nat, w, tiles, factor in ((2, nat_down, down_w, HT, 0.5), (3, nat_out, out_w, OT, 1.0)):
            for m in range(0, tiles, 2):
                weight_groups.append((which, [nat[:, k, (m + i) * P:(m + i + 1) * P]
                                              for i in range(2) for k in range(KD)],
                                      w[:, HIGH, m:m + 2, :], w[:, LOW, m:m + 2, :], factor))

        def bank_of(n, blocks):
            return (G + U)[n % 4][:, 0:len(blocks) * P]

        def shaped(bank, like):
            return bank if len(like.shape) == 2 else bank.rearrange("p (n c) -> p n c", n=2)

        block = ctx.enter_context(nc.Block())

        def batches(eng, program):
            program(0, FIRST)
            with eng.Fori(1, BATCH - 1) as b:
                program(b, MIDDLE)
            program(BATCH - 1, LAST)

        @block.sync
        def _(sp):
            def rows(t, b, n):
                return t[bass.ds(b * n, n), :]

            def load_x(b):
                sp.dma_start(xb[:, :, :], rows(x, b, SEQ).rearrange("(n p) d -> p n d", p=P)).then_inc(x_loaded, 16)

            load_x(0)
            for n, (tile, src) in enumerate(((raw_gate, w_gate), (raw_up, w_up), (raw_down, w_down), (nat_out, W_out))):
                sp.dma_start(tile[:, :, :], src.rearrange("(n p) d -> p n d", p=P)).then_inc(w_loaded[n], 16)

            def program(b, part):
                if part != FIRST:
                    sp.wait_ge(y_done, 2 * b)
                    sp.sem_inc(ticks, 1)
                sp.dma_start(xres[:, :, :], rows(x, b, SEQ).rearrange("(n p) d -> p n d", p=P)).then_inc(xres_loaded, 16)
                if part != FIRST:
                    sp.wait_ge(o_low, b)
                    sp.sem_inc(ticks, 1)
                sp.dma_start(o_in[:, :, :], rows(heads_out, b, INNER).rearrange("(n p) d -> p n d", p=P)).then_inc(o_loaded, 16)
                if part != LAST:
                    sp.wait_ge(xT_low, b * KD + KD)
                    sp.sem_inc(ticks, 1)
                    load_x(b + 1)
                sp.wait_ge(y_done, 2 * b + 2)
                sp.sem_inc(ticks, 1)
                sp.dma_start(rows(out, b, SEQ).rearrange("(n p) d -> p n d", p=P), y_s[:, :, :]).then_inc(y_stored, 16)

            batches(sp, program)
            sp.wait_ge(y_stored, 16 * BATCH)

        @block.gpsimd
        def _(pool):
            pool.memset(ident[:, :], 0.0).then_inc(zeroed, 1)
            pool.memset(minus_half[:, :], -0.5).then_inc(consts, 1)
            pool.wait_ge(zeroed, 1)
            pool.affine_select(out=ident[:, :], in_=ident[:, :], compare_op=ALU.not_equal, fill=1.0,
                               base=0, pattern=[[-1, P]], channel_multiplier=1).then_inc(consts, 1)
            pool.wait_ge(consts, 2)

            def rstd_of(b):
                pool.wait_ge(var_done, b + 1)
                pool.tensor_tensor(rstd[:, :], var_eps[:, :], minus_half[:, :], ALU.pow).then_inc(rstd_done, 1)

            rstd_of(0)

            def program(b, part):
                if part != LAST:
                    rstd_of(b + 1)

            batches(pool, program)

        @block.tensor
        def _(pe):
            pe.wait_ge(consts, 2)
            for n, (which, blocks, _, _, _) in enumerate(weight_groups):
                if which < 3:
                    pe.wait_ge(dequantized, which + 1)
                else:
                    pe.wait_ge(w_loaded[3], 16)
                if n >= 4:
                    pe.wait_ge(w_low, n - 3)
                for i, source in enumerate(blocks):
                    last = pe.transpose(bank_of(n, blocks)[:, i * P:(i + 1) * P], source, ident[:, :])
                last.then_inc(w_turned, 1)

            def transpose_x(b):
                pe.wait_ge(xn_done, b + 1)
                if not (isinstance(b, int) and b == 0):
                    pe.wait_ge(xT_low, b * KD)
                for k in range(KD):
                    for n in range(TT):
                        last = pe.transpose(XT[k][:, n * P:(n + 1) * P], xb[:, n, k * P:(k + 1) * P], ident[:, :])
                    last.then_inc(xT_filled, 1)

            def gate_up(b, m):
                if not (isinstance(b, int) and b * HT + m < 2):
                    pe.wait_ge(hidden_done, b * HT + m - 1)
                for bank, w in ((G[m % 2], gate_w), (U[m % 2], up_w)):
                    n = 0
                    for k in range(KD):
                        for a, c in PRODUCTS:
                            last = pe.matmul(bank[:, :], w[:, a, k, m * P:(m + 1) * P], xT[:, c, k, :],
                                             start=(n == 0), stop=(n == 3 * KD - 1))
                            n += 1
                last.then_inc(gu_filled, 1)

            def into_y(parts, w, m, begin, end):
                for t in range(TT):
                    for n, (a, c) in enumerate(PRODUCTS):
                        last = pe.matmul(Y[t // 2][:, (t % 2) * DIM:(t % 2 + 1) * DIM],
                                         parts[:, a, m, t * P:(t + 1) * P], w[:, c, m, :],
                                         start=(begin and n == 0 and t % 2 == 0), stop=(end and n == 2),
                                         skip_group_check=True)
                    if end and t % 2 == 1:
                        last.then_inc(y_filled, 1)

            def down(b, m):
                if m == 0 and not (isinstance(b, int) and b == 0):
                    pe.wait_ge(y_done, 2 * b)
                pe.wait_ge(h_low, b * HT + m + 1)
                into_y(h_s, down_w, m, m == 0, m == HT - 1)

            def program(b, part):
                pe.wait_ge(xT_low, b * KD + KD)
                for m in range(HT):
                    gate_up(b, m)
                    if m >= 2:
                        down(b, m - 2)
                if part != LAST:
                    transpose_x(b + 1)
                pe.wait_ge(o_low, b + 1)
                for m in range(OT):
                    into_y(o_s, out_w, m, False, False)
                down(b, HT - 2)
                down(b, HT - 1)

            pe.wait_ge(w_low, len(weight_groups))
            transpose_x(0)
            batches(pe, program)

        @block.scalar
        def _(act):
            for n, (which, blocks, high, _, factor) in enumerate(weight_groups):
                act.wait_ge(w_turned, n + 1)
                act.activation(high, shaped(bank_of(n, blocks), high), ACT.Copy, scale=factor).then_inc(w_high, 1)

            def high_xT(b):
                for k in range(KD):
                    act.wait_ge(xT_filled, b * KD + k + 1)
                    act.activation(xT[:, HIGH, k, :], XT[k][:, :], ACT.Copy).then_inc(xT_high, 1)

            def tanh_of(b, m):
                act.wait_ge(gu_filled, b * HT + m + 1)
                if not (isinstance(b, int) and b * HT + m < 2):
                    act.wait_ge(h_low, b * HT + m - 1)
                act.activation(act_s[:, m % 2, :], G[m % 2][:, :], ACT.Tanh, scale=0.5).then_inc(tanh_done, 1)

            def high_h(b, m):
                act.wait_ge(hidden_done, b * HT + m + 1)
                act.activation(h_s[:, HIGH, m, :], act_s[:, m % 2, :], ACT.Copy).then_inc(h_high, 1)

            def high_o(b):
                act.wait_ge(o_loaded, b * 16 + 16)
                act.activation(o_s[:, HIGH, :, :], o_in[:, :, :], ACT.Copy).then_inc(o_high, 1)

            def program(b, part):
                for m in range(HT):
                    tanh_of(b, m)
                    if m >= 1:
                        high_h(b, m - 1)
                    if m == 2:
                        high_o(b)
                high_h(b, HT - 1)
                if part != LAST:
                    high_xT(b + 1)

            high_xT(0)
            batches(act, program)

        @block.vector
        def _(dve):
            def x_norm(nb):
                for n in range(TT):
                    if n == 0:
                        dve.wait_ge(x_loaded, nb * 16 + 16)
                    last = dve.bn_stats(stats[:, n, :], xb[:, n, :])
                last.then_inc(stats_done, 1)
                wait_before(dve, stats_done, nb + 1)
                for n in range(TT):
                    last = dve.bn_aggr(mean_var[:, n, :], stats[:, n, :])
                last.then_inc(agg_done, 1)
                dve.wait_ge(agg_done, nb + 1)
                dve.tensor_scalar(var_eps[:, :], mean_var[:, :, 1], EPS, None, ALU.add).then_inc(var_done, 1)

            def x_scale(nb):
                for n in range(TT):
                    if n == 0:
                        dve.wait_ge(rstd_done, nb + 1)
                    last = dve.tensor_scalar(xb[:, n, :], xb[:, n, :], mean_var[:, n, 0:1], rstd[:, n:n + 1],
                                             ALU.subtract, ALU.mult)
                last.then_inc(xn_done, 1)

            def low_xT(b):
                for k in range(KD):
                    dve.wait_ge(xT_high, b * KD + k + 1)
                    dve.tensor_tensor(xT[:, LOW, k, :], XT[k][:, :], xT[:, HIGH, k, :].bitcast(F32), ALU.subtract) \
                       .then_inc(xT_low, 1)

            def hidden(b, m):
                a = act_s[:, m % 2, :]
                dve.wait_ge(tanh_done, b * HT + m + 1)
                dve.scalar_tensor_tensor(a, a, 1.0, G[m % 2][:, :], ALU.add, ALU.mult).then_inc(gated, 1)
                dve.wait_ge(gated, b * HT + m + 1)
                dve.tensor_tensor(a, a, U[m % 2][:, :], ALU.mult).then_inc(hidden_done, 1)

            def low_h(b, m):
                dve.wait_ge(h_high, b * HT + m + 1)
                dve.tensor_tensor(h_s[:, LOW, m, :], act_s[:, m % 2, :], h_s[:, HIGH, m, :].bitcast(F32),
                                  ALU.subtract).then_inc(h_low, 1)

            def low_o(b):
                dve.wait_ge(o_high, b + 1)
                dve.tensor_tensor(o_s[:, LOW, :, :], o_in[:, :, :], o_s[:, HIGH, :, :].bitcast(F32),
                                  ALU.subtract).then_inc(o_low, 1)

            def sum_y(b):
                for i in range(2):
                    dve.wait_ge(y_filled, 2 * b + i + 1)
                    if i == 0:
                        dve.wait_ge(xres_loaded, b * 16 + 16)
                        if not (isinstance(b, int) and b == 0):
                            dve.wait_ge(y_stored, b * 16)
                    dve.tensor_tensor(y_s[:, 2 * i:2 * i + 2, :], Y[i][:, :].rearrange("p (n c) -> p n c", n=2),
                                      xres[:, 2 * i:2 * i + 2, :], ALU.add).then_inc(y_done, 1)

            def program(b, part):
                for m in range(HT):
                    hidden(b, m)
                    if m >= 1:
                        low_h(b, m - 1)
                    if m == 1 and part != LAST:
                        x_norm(b + 1)
                    if m == 3:
                        low_o(b)
                    if m == 4 and part != LAST:
                        x_scale(b + 1)
                low_h(b, HT - 1)
                if part != LAST:
                    low_xT(b + 1)
                sum_y(b)

            x_norm(0)
            for n, (nat, raw) in enumerate(((nat_gate, raw_gate), (nat_up, raw_up), (nat_down, raw_down))):
                dve.wait_ge(w_loaded[n], 16)
                dve.tensor_scalar(nat[:, :, :], raw[:, :, :], 1.0 / 127.0, None, ALU.mult).then_inc(dequantized, 1)
            x_scale(0)
            for n, (which, blocks, high, low, factor) in enumerate(weight_groups):
                dve.wait_ge(w_high, n + 1)
                dve.scalar_tensor_tensor(low, shaped(bank_of(n, blocks), low), factor, high.bitcast(F32),
                                         ALU.mult, ALU.subtract).then_inc(w_low, 1)
            low_xT(0)
            batches(dve, program)


def build(nc, x, W_qkv, W_out, w_gate, w_up, w_down, out):
    x_rows = x.rearrange("b n d -> (b n) d")
    out_rows = out.rearrange("b n d -> (b n) d")
    heads_out = nc.dram_tensor("heads_out", [BATCH * INNER, SEQ], F32).ap()
    with ExitStack() as ctx:
        W_high = ctx.enter_context(nc.sbuf_tensor("W_high", [P, KD, 6 * INNER], F32R))
        W_low = ctx.enter_context(nc.sbuf_tensor("W_low", [P, KD, 6 * INNER], F32R))
        split_weights(nc, W_qkv, W_high, W_low)
        attention(nc, x_rows, W_high, W_low, heads_out)
    ffn_and_sum(nc, x_rows, w_gate, w_up, w_down, W_out, heads_out, out_rows)


_INS = ["L0_attn_x", "L0_attn_W_qkv", "L0_attn_W_out", "L0_ffn_w_gate", "L0_ffn_w_up", "L0_ffn_w_down"]


def kernel(**inputs):
    import concourse.bacc as bacc
    from concourse.bass_utils import run_bass_kernel_spmd

    nc = bacc.Bacc("TRN2", target_bir_lowering=False, num_devices=1)
    arrays, args = {}, []
    for name in _INS:
        a = np.ascontiguousarray(inputs[name])
        arrays[f"in_{name}"] = a
        args.append(nc.dram_tensor(f"in_{name}", a.shape, mybir.dt.from_np(a.dtype), kind="ExternalInput").ap())
    out = nc.dram_tensor("out", (BATCH, SEQ, DIM), F32, kind="ExternalOutput").ap()
    build(nc, *args, out)
    r = run_bass_kernel_spmd(nc, [arrays], core_ids=[0])
    return r.results[0]["out"]
```

```python
import numpy as np
import concourse.bass as bass
from concourse import mybir
from contextlib import ExitStack

F32 = mybir.dt.float32
F32R = mybir.dt.float32r
I32 = mybir.dt.int32
ALU = mybir.AluOpType
ACT = mybir.ActivationFunctionType

P = 128
BATCH, SEQ, DIM = 8, 512, 256
HEADS, DH = 8, 64
INNER = HEADS * DH
HIDDEN = 768
KD = DIM // P
TT = SEQ // P
HT = HIDDEN // P
OT = INNER // P
PAIRS = HEADS // 2
EPS = 1e-5
QU, KU, VU, QC, KC, VC = range(6)
W_ORDER = (QC, KC, QU, KU, VU, VC)
X_AFTER = 4

TRI = 1280
GROUP = [(0, 512), (512, 512), (1024, 256)]
WIDE = {4: 0, 3: 512, 1: 896, 2: 1024}
ROWS = [(4,), (3, 1), (2,)]
HIGH, LOW = 0, 1
PRODUCTS = [(HIGH, HIGH), (HIGH, LOW), (LOW, HIGH)]

LOOK_SCALE = 1.0 / 16
SU_SCALE = 1.0 / 32
KC_FACTOR = -4.0
MASKED = 2.0 ** 100
INT_SCALE = 1.0 / 127.0
HIDDEN_SCALE = 0.5 * INT_SCALE ** 3
NO_SCORE = 3.0e38


class Shared:

    def __init__(self, nc, ctx):
        def sb(name, shape, dt):
            return ctx.enter_context(nc.sbuf_tensor(name, shape, dt))

        self.ident = sb("ident", [P, P], F32)
        self.minus_half = sb("minus_half", [P, TT], F32)
        self.xb = sb("xb", [P, TT, DIM], F32)
        self.stats = sb("stats", [P, TT, 6], F32)
        self.mean_var = sb("mean_var", [P, TT, 2], F32)
        self.var_eps = sb("var_eps", [P, TT], F32)
        self.rstd = sb("rstd", [P, TT], F32)
        self.xT = sb("xT", [P, 2, KD, SEQ], F32R)
        self.W = sb("W", [P, 2, KD, 6 * INNER], F32R)
        self.o_stored = [ctx.enter_context(nc.semaphore(f"o_stored{i}")) for i in range(2)]
        self.has_low = sb("has_low", [1, 1], I32)
        words = self.W[:, :, :, :].rearrange("p a k c -> p (a k c)")
        size = 2 * KD * HIDDEN
        self.gate_w = words[:, 0:size].rearrange("p (a k h) -> p a k h", a=2, k=KD)
        self.up_w = words[:, size:2 * size].rearrange("p (a k h) -> p a k h", a=2, k=KD)
        self.down_w = words[:, 2 * size:3 * size].rearrange("p (a m d) -> p a m d", a=2, m=HT)
        self.out_w = words[:, 3 * size:3 * size + 2 * OT * DIM].rearrange("p (a m d) -> p a m d", a=2, m=OT)


class LayerNorm:

    def __init__(self, nc, ctx, tag, sh, first, ticks):
        self.sh, self.first, self.ticks = sh, first, ticks
        self.loaded, self.stats_done, self.agg_done, self.var_done, self.rstd_done, self.done = (
            ctx.enter_context(nc.semaphore(f"{tag}_{name}"))
            for name in ("x_loaded", "stats_done", "agg_done", "var_done", "rstd_done", "xn_done"))

    def load(self, sp, x, b):
        sp.dma_start(self.sh.xb[:, :, :], x[bass.ds(b * SEQ, SEQ), :].rearrange("(n p) d -> p n d", p=P)) \
          .then_inc(self.loaded, 16)

    def take_stats(self, dve, b):
        sh, nth = self.sh, b - self.first + 1
        for n in range(TT):
            if n == 0:
                dve.wait_ge(self.loaded, nth * 16)
            last = dve.bn_stats(sh.stats[:, n, :], sh.xb[:, n, :])
        last.then_inc(self.stats_done, 1)
        dve.wait_ge(self.stats_done, nth)
        dve.sem_inc(self.ticks, 1)
        for n in range(TT):
            last = dve.bn_aggr(sh.mean_var[:, n, :], sh.stats[:, n, :])
        last.then_inc(self.agg_done, 1)
        dve.wait_ge(self.agg_done, nth)
        dve.tensor_scalar(sh.var_eps[:, :], sh.mean_var[:, :, 1], EPS, None, ALU.add).then_inc(self.var_done, 1)

    def take_rstd(self, pool, b):
        pool.wait_ge(self.var_done, b - self.first + 1)
        pool.tensor_tensor(self.sh.rstd[:, :], self.sh.var_eps[:, :], self.sh.minus_half[:, :], ALU.pow) \
            .then_inc(self.rstd_done, 1)

    def scale(self, dve, b):
        sh = self.sh
        for n in range(TT):
            if n == 0:
                dve.wait_ge(self.rstd_done, b - self.first + 1)
            last = dve.tensor_scalar(sh.xb[:, n, :], sh.xb[:, n, :], sh.mean_var[:, n, 0:1], sh.rstd[:, n:n + 1],
                                     ALU.subtract, ALU.mult)
        last.then_inc(self.done, 1)


def prologue(nc, x, W_qkv, sh):
    tiles = 6 * INNER // P
    per = SEQ // P
    groups = 6 * KD
    ctx = ExitStack()
    with ctx:
        def sem(name):
            return ctx.enter_context(nc.semaphore(name))

        raw = ctx.enter_context(nc.sbuf_tensor("w_raw", [P, tiles, DIM], F32))
        banks = [ctx.enter_context(nc.psum_tensor(f"w_bank{i}", [P, 512], F32)) for i in range(6)]
        x_banks = [ctx.enter_context(nc.psum_tensor(f"x_bank{i}", [P, 512], F32)) for i in range(KD)]
        loaded = [sem(f"w_loaded{i}") for i in range(6)]
        zeroed = sem("w_zeroed")
        ident_ready = sem("w_ident_ready")
        turned = sem("w_turned")
        high_done = sem("w_high_done")
        low_done = sem("w_low_done")
        x_turned = sem("w_x_turned")
        x_high_done = sem("w_x_high_done")
        x_low_done = sem("w_x_low_done")
        ticks = sem("w_ticks")
        norm = LayerNorm(nc, ctx, "w", sh, 0, ticks)
        block = ctx.enter_context(nc.Block())

        @block.sync
        def _(sp):
            norm.load(sp, x, 0)
            for t in W_ORDER:
                sp.dma_start(raw[:, per * t:per * (t + 1), :],
                             W_qkv[t * INNER:(t + 1) * INNER, :].rearrange("(n p) d -> p n d", p=P)) \
                  .then_inc(loaded[t], 16)

        @block.gpsimd
        def _(pool):
            pool.memset(sh.ident[:, :], 0.0).then_inc(zeroed, 1)
            pool.memset(sh.minus_half[:, :], -0.5).then_inc(zeroed, 1)
            pool.wait_ge(zeroed, 2)
            pool.affine_select(out=sh.ident[:, :], in_=sh.ident[:, :], compare_op=ALU.not_equal, fill=1.0,
                               base=0, pattern=[[-1, P]], channel_multiplier=1).then_inc(ident_ready, 1)
            norm.take_rstd(pool, 0)

        @block.tensor
        def _(pe):
            pe.wait_ge(ident_ready, 1)
            for n in range(groups):
                t, k = W_ORDER[n // KD], n % KD
                if n == X_AFTER:
                    pe.wait_ge(norm.done, 1)
                    for c in range(KD):
                        for i in range(TT):
                            last = pe.transpose(x_banks[c][:, i * P:(i + 1) * P],
                                                sh.xb[:, i, c * P:(c + 1) * P], sh.ident[:, :])
                        last.then_inc(x_turned, 1)
                if k == 0:
                    pe.wait_ge(loaded[t], 16)
                if n >= 6:
                    pe.wait_ge(low_done, n - 5)
                for i in range(per):
                    last = pe.transpose(banks[n % 6][:, i * P:(i + 1) * P],
                                        raw[:, per * t + i, k * P:(k + 1) * P], sh.ident[:, :])
                last.then_inc(turned, 1)

        @block.scalar
        def _(act):
            for n in range(groups):
                t, k = W_ORDER[n // KD], n % KD
                if n == X_AFTER:
                    for c in range(KD):
                        act.wait_ge(x_turned, c + 1)
                        act.activation(sh.xT[:, HIGH, c, :], x_banks[c][:, :], ACT.Copy).then_inc(x_high_done, 1)
                act.wait_ge(turned, n + 1)
                act.activation(sh.W[:, HIGH, k, t * INNER:(t + 1) * INNER], banks[n % 6][:, :], ACT.Copy,
                               scale=KC_FACTOR if t == KC else 1.0).then_inc(high_done, 1)

        @block.vector
        def _(dve):
            norm.take_stats(dve, 0)
            norm.scale(dve, 0)
            for n in range(groups):
                t, k = W_ORDER[n // KD], n % KD
                if n == X_AFTER:
                    for c in range(KD):
                        dve.wait_ge(x_high_done, c + 1)
                        dve.tensor_tensor(sh.xT[:, LOW, c, :], x_banks[c][:, :], sh.xT[:, HIGH, c, :].bitcast(F32),
                                          ALU.subtract).then_inc(x_low_done, 1)
                dve.wait_ge(high_done, n + 1)
                dve.scalar_tensor_tensor(sh.W[:, LOW, k, t * INNER:(t + 1) * INNER], banks[n % 6][:, :],
                                         KC_FACTOR if t == KC else 1.0,
                                         sh.W[:, HIGH, k, t * INNER:(t + 1) * INNER].bitcast(F32),
                                         ALU.mult, ALU.subtract).then_inc(low_done, 1)


X_BANKS = 4
PROJ_ORDER = [QC, KC, QU, KU, VU]
FIRST_PAIR = [QU, KU, QC, VU, KC]
FIRST, MIDDLE, LAST = range(3)

W_GROUPS = [(w, k, a, b) for w in range(2) for k in range(KD) for a, b in ((0, 4), (4, HT))]
W_GROUPS += [(2, m, 0, KD) for m in range(0, HT, 2)] + [(3, m, 0, KD) for m in range(0, OT, 2)]
WEIGHTS_IN_STEP = {6: range(0, 4), 7: range(4, 6)}
FINISH = [("W", HEADS, 6), ("W", HEADS, 7), ("PT", HEADS, 0), ("PT", HEADS, 1), ("PT", HEADS, 2), ("O", HEADS, 0)]
FINISH += [("W", HEADS, n) for n in range(8, 11)]
FINISH += [("PT", HEADS + 1, 0), ("PT", HEADS + 1, 1), ("PT", HEADS + 1, 2)]
FINISH += [("W", HEADS, 11), ("W", HEADS, 12), ("O", HEADS + 1, 0)]

X_ORDER = [
    [("L", 0), ("L", 1), ("PT", 0), ("PT", 1), ("PT", 2), ("L", 2), ("T", 0), ("XT", 0), ("XT", 1),
     ("O", 0), ("T", 1), ("T", 2), ("proj", QC), ("V", 0), ("proj", KC)],
    [("L", 0), ("L", 1), ("PT", 0), ("L", 2), ("proj", QU), ("PT", 1), ("T", 0), ("PT", 2), ("T", 1),
     ("O", 0), ("T", 2), ("proj", KU), ("proj", VU)],
]


def x_groups(s, part):
    ahead = s < 6 or part != LAST
    there = {"L": True, "T": True, "PT": s >= 2 or part != FIRST, "O": s >= 2 or part != FIRST,
             "XT": s == 6, "proj": ahead, "V": ahead}
    out = [(kind, s, n) for kind, n in X_ORDER[s % 2] if there[kind]]
    if part == LAST:
        out += [("W", s, n) for n in WEIGHTS_IN_STEP.get(s, ())]
    return out


def x_schedule():
    orders = []
    for part in (FIRST, MIDDLE, LAST):
        order = []
        if part == FIRST:
            order += [("proj", -2, t) for t in FIRST_PAIR] + [("V", -2, 0)]
        for s in range(HEADS):
            order += x_groups(s, part)
        if part == LAST:
            order += FINISH
        orders.append(order)
    shift = [(len(orders[MIDDLE]) - len(orders[FIRST])) % X_BANKS, 0, 0]
    held = {(n + len(orders[MIDDLE])) % X_BANKS: key for n, key in enumerate(orders[MIDDLE][-X_BANKS:], -X_BANKS)}
    parts = []
    for part, order in enumerate(orders):
        had, found = [0] * X_BANKS, {}
        before = {} if part == FIRST else {bank: (key, 1) for bank, key in held.items()}
        for n, key in enumerate(order):
            bank = (n + shift[part]) % X_BANKS
            had[bank] += 1
            found[key] = (bank, had[bank], before.get(bank))
            before[bank] = (key, 0)
        parts.append((found, had))
        if part < LAST:
            assert {bank: key for bank, (key, _) in before.items()} == held
    return parts


X_PLAN = x_schedule()


def attention(nc, x, w_gate, w_up, w_down, W_out, sh, heads_out):
    ctx = ExitStack()
    with ctx:
        def sb(name, shape, dt):
            return ctx.enter_context(nc.sbuf_tensor(name, shape, dt))

        def pb(name):
            return ctx.enter_context(nc.psum_tensor(name, [P, 512], F32))

        def sem(name):
            return ctx.enter_context(nc.semaphore(name))

        ident, xb, xT = sh.ident, sh.xb, sh.xT
        ku_s = sb("ku_s", [P, 2, SEQ], F32R)
        vu_s = sb("vu_s", [P, 2, SEQ], F32R)
        kc_s = sb("kc_s", [P, 2, 2, SEQ], F32R)
        qu_s = sb("qu_s", [P, 2, 2, SEQ], F32R)
        qc_s = sb("qc_s", [P, 2, 2, 2, SEQ], F32R)
        v_s = sb("v_s", [P, 2, TT, 4, 2, DH], F32R)
        tanh_l = sb("tanh_l", [P, TRI], F32)
        L_s = sb("L_s", [P, 2, 2, TRI], F32R)
        T_s = sb("T_s", [P, 2, 2, TRI], F32R)
        gate = sb("gate", [P, TRI], F32)
        prob = sb("prob", [P, 2, TRI], F32)
        least = sb("least", [P, 2, 4], F32)
        total = sb("total", [P, 2, 4], F32)
        inv = sb("inv", [P, 2, 4], F32)
        PT_s = sb("PT_s", [P, 2, TRI], F32R)
        o_low = sb("o_low", [DH, SEQ], F32)
        o_s = sb("o_s", [P, 2, SEQ], F32)
        int_gate = sb("int_gate", [P, HT, DIM], I32)
        int_up = sb("int_up", [P, HT, DIM], I32)
        int_down = int_gate[:, :, :].rearrange("p n c -> p (n c)").rearrange("p (n c) -> p n c", n=KD)
        raw_out = xb[:, :, :].rearrange("p n c -> p (n c)").rearrange("p (n c) -> p n c", n=KD)
        low_max = sb("low_max", [P, 3], F32)
        low_row = sb("low_row", [1, 3 * P], F32)
        largest = sb("largest", [1, 1], F32)
        natural = [int_gate[:, :, :].bitcast(F32), int_up[:, :, :].bitcast(F32), int_down.bitcast(F32), raw_out]
        placed = [sh.gate_w, sh.up_w, sh.down_w, sh.out_w]

        X = [pb(f"X{i}") for i in range(X_BANKS)]
        Su = [pb(f"Su{i}") for i in range(2)]
        Sc = [pb(f"Sc{i}") for i in range(2)]

        x_filled = [sem(f"x_filled{i}") for i in range(X_BANKS)]
        xT_high = sem("xT_high")
        xT_low = sem("xT_low")
        proj_high = sem("proj_high")
        proj_low = sem("proj_low")
        qc_twice = sem("qc_twice")
        qu_twice = sem("qu_twice")
        v_high = sem("v_high")
        v_low = sem("v_low")
        tanh_done = sem("tanh_done")
        tanh_masked = sem("tanh_masked")
        L_high = sem("L_high")
        L_ready = sem("L_ready")
        T_high = sem("T_high")
        T_low = sem("T_low")
        T_ready = sem("T_ready")
        scores_filled = sem("scores_filled")
        gate_done = sem("gate_done")
        silu_done = sem("silu_done")
        silu_masked = sem("silu_masked")
        scores_emptied = sem("scores_emptied")
        exp_done = sem("exp_done")
        inv_done = sem("inv_done")
        prob_ready = sem("prob_ready")
        PT_high = sem("PT_high")
        PT_low = sem("PT_low")
        o_low_copied = sem("o_low_copied")
        o_copied = sem("o_copied")
        o_stored = sh.o_stored
        w_loaded = [sem(f"w_loaded{i}") for i in range(4)]
        made_float = sem("made_float")
        low_max_taken = sem("low_max_taken")
        low_max_gathered = sem("low_max_gathered")
        largest_taken = sem("largest_taken")
        w_high = sem("w_high")
        w_low = sem("w_low")
        ticks = sem("ticks")
        ln = LayerNorm(nc, ctx, "a", sh, 1, ticks)

        def x_before(part, b, bank):
            n0, n1 = X_PLAN[FIRST][1][bank], X_PLAN[MIDDLE][1][bank]
            return 0 if part == FIRST else (b - 1) * n1 + n0 if part == MIDDLE else (BATCH - 2) * n1 + n0

        def x_use(part, b, key):
            bank, nth, _ = X_PLAN[part][0][key]
            return bank, x_before(part, b, bank) + nth

        def wait_before(eng, signal, value):
            eng.wait_ge(signal, value)
            eng.sem_inc(ticks, 1)

        def after(n, per, j):
            return n * per + j + 1

        def proj_count(q, t):
            if isinstance(q, int) and q == 0:
                return FIRST_PAIR.index(t) + 1
            return q * 5 + PROJ_ORDER.index(t) + 1

        def v_count(b, s):
            return b * 4 + s // 2 + 2

        def v_piece(s):
            return (s + 2) // 4 % 2, (s // 2 + 1) % 2

        def weight_group(n):
            w, m, a, b = W_GROUPS[n]
            if w < 2:
                blocks = [natural[w][:, i, m * P:(m + 1) * P] for i in range(a, b)]
                return w, blocks, [placed[w][:, c, m, a * P:b * P] for c in (HIGH, LOW)]
            blocks = [natural[w][:, k, (m + i) * P:(m + i + 1) * P] for i in range(2) for k in range(KD)]
            return w, blocks, [placed[w][:, c, m:m + 2, :] for c in (HIGH, LOW)]

        def shaped(bank, blocks, like):
            v = bank[:, 0:len(blocks) * P]
            return v if len(like.shape) == 2 else v.rearrange("p (n c) -> p n c", n=2)

        def x_read(b, key):
            kind, s, n = key
            if kind == "XT":
                return xT_low, after(b, KD, n)
            if kind == "W":
                return w_low, n + 1
            if kind == "L":
                return tanh_done, after(b * HEADS + s, 3, n)
            if kind == "T":
                return T_low, after(b * HEADS + s, 3, n)
            if kind == "PT":
                return PT_low, after(b * HEADS + s - 2, 3, n)
            if kind == "O":
                return o_copied, b * HEADS + s - 1
            if kind == "V":
                return v_low, v_count(b, s)
            return proj_low, proj_count(b * PAIRS + s // 2 + 1, n)

        block = ctx.enter_context(nc.Block())

        def batches(eng, program):
            program(0, FIRST)
            with eng.Fori(1, BATCH - 1) as b:
                program(b, MIDDLE)
            program(BATCH - 1, LAST)

        def run_steps(b, part, even_step, odd_step):
            for s in range(HEADS):
                back1 = s >= 1 or part != FIRST
                back2 = s >= 2 or part != FIRST
                ahead = s < 6 or part != LAST
                step = odd_step if s % 2 else even_step
                step(part, b, s, b * HEADS + s, (s - 1) % HEADS, back1, back2, ahead)

        @block.sync
        def _(sp):
            def load_weight(n, tile, src):
                sp.dma_start(tile, src.rearrange("(n p) d -> p n d", p=P)).then_inc(w_loaded[n], 16)

            def program(b, part):
                for s in range(HEADS + (2 if part == LAST else 0)):
                    g = b * HEADS + s
                    if s == 0:
                        if part != FIRST:
                            sp.wait_ge(xT_low, b * KD)
                            sp.sem_inc(ticks, 1)
                        ln.load(sp, x, 0 if part == LAST else b + 1)
                    if part == LAST and s == 0:
                        load_weight(0, int_gate[:, :, :], w_gate)
                        load_weight(1, int_up[:, :, :], w_up)
                    if part == LAST and s == 7:
                        sp.wait_ge(xT_low, BATCH * KD)
                        load_weight(3, raw_out, W_out)
                        sp.wait_ge(w_low, 4)
                        load_weight(2, int_down, w_down)
                    if part == LAST and s == 9:
                        sp.wait_ge(low_max_taken, 3)
                        sp.dma_start(low_row[:, :], low_max[:, :]).then_inc(low_max_gathered, 16)
                    if s < HEADS and (s < 6 or part != LAST):
                        q = b * PAIRS + s // 2 + 1
                        if s % 2 == 0:
                            dup(QC, q, (s // 2 + 1) % 2)
                        else:
                            dup(QU, q, 0)
                    if s >= 2 or part != FIRST:
                        if s % 2 == 1:
                            par = ((s - 3) // 2) % 2
                            sp.wait_ge(o_copied, g - 1)
                            sp.sem_inc(ticks, 1)
                            sp.dma_start(heads_out[bass.ds((b * PAIRS + (s - 3) // 2) * P, P), :],
                                         o_s[:, par, :]).then_inc(o_stored[par], 16)
                if part == LAST:
                    sp.wait_ge(o_stored[0], 16 * (BATCH - 1) * PAIRS // 2)
                    sp.wait_ge(o_stored[1], 16 * (BATCH - 1) * PAIRS // 2)

            def dup(t, q, par):
                sp.wait_ge(proj_low, proj_count(q, t))
                sp.sem_inc(ticks, 1)
                tile, done = (qc_s[:, par], qc_twice) if t == QC else (qu_s[:, :], qu_twice)
                words = tile.bitcast(F32)
                sp.dma_start(words[DH:P, 0, :, :], words[0:DH, 0, :, :]).then_inc(done, 16)
                sp.dma_start(words[0:DH, 1, :, :], words[DH:P, 1, :, :]).then_inc(done, 16)

            dup(QU, 0, 0)
            dup(QC, 0, 0)
            batches(sp, program)

        @block.gpsimd
        def _(pool):
            def mask_silu(g, s, j):
                wait_before(pool, silu_done, after(g, 3, j))
                first, n = [(WIDE[4] + 384, 1), (WIDE[3] + 256, 2), (WIDE[2] + 128, 1)][j]
                v = gate[:, first:first + n * P].rearrange("p (n c) -> p n c", n=n)
                pool.affine_select(out=v, in_=v, compare_op=ALU.is_ge, fill=MASKED, base=0,
                                   pattern=[[0, n], [-1, P]], channel_multiplier=1).then_inc(silu_masked, 1)

            def mask_tanh(g, j):
                wait_before(pool, tanh_done, after(g, 3, j))
                first, n = [(WIDE[4] + 384, 1), (WIDE[3] + 256, 2), (WIDE[2] + 128, 1)][j]
                v = tanh_l[:, first:first + n * P].rearrange("p (n c) -> p n c", n=n)
                pool.affine_select(out=v, in_=v, compare_op=ALU.is_ge, fill=-1.0, base=-1,
                                   pattern=[[0, n], [-1, P]], channel_multiplier=1).then_inc(tanh_masked, 1)

            def mask_T(g, par, j):
                wait_before(pool, T_low, after(g, 3, j))
                for i, w in enumerate(ROWS[j]):
                    v = T_s[:, par, :, WIDE[w]:WIDE[w] + P]
                    last = pool.affine_select(out=v, in_=v.bitcast(F32), compare_op=ALU.is_ge, fill=0.0,
                                              base=0, pattern=[[0, 2], [1, P]], channel_multiplier=-1)
                last.then_inc(T_ready, 1)

            def norm(g, s, j):
                hp = s % 2
                wait_before(pool, inv_done, after(g, 3, j))
                for w in ROWS[j]:
                    v = prob[:, hp, WIDE[w]:WIDE[w] + w * P]
                    last = pool.tensor_scalar(v, v, inv[:, hp, w - 1:w], None, ALU.mult)
                last.then_inc(prob_ready, 1)

            def even_step(part, b, s, g, s1, back1, back2, ahead):
                if back1:
                    mask_silu(g - 1, s1, 0)
                mask_tanh(g, 0)
                mask_tanh(g, 1)
                if back1:
                    mask_silu(g - 1, s1, 1)
                mask_T(g, s % 2, 0)
                mask_tanh(g, 2)
                if back1:
                    norm(g - 1, s1, 0)
                    mask_silu(g - 1, s1, 2)
                mask_T(g, s % 2, 1)
                mask_T(g, s % 2, 2)
                if back1:
                    norm(g - 1, s1, 1)
                    norm(g - 1, s1, 2)
                if s == 4:
                    ln.take_rstd(pool, b + 1)

            def odd_step(part, b, s, g, s1, back1, back2, ahead):
                mask_tanh(g, 0)
                mask_tanh(g, 1)
                if back1:
                    mask_silu(g - 1, s1, 0)
                mask_tanh(g, 2)
                if back1:
                    mask_silu(g - 1, s1, 1)
                    norm(g - 1, s1, 0)
                    mask_silu(g - 1, s1, 2)
                mask_T(g, s % 2, 0)
                mask_T(g, s % 2, 1)
                mask_T(g, s % 2, 2)
                if back1:
                    norm(g - 1, s1, 1)
                    norm(g - 1, s1, 2)

            def program(b, part):
                run_steps(b, part, even_step, odd_step)

            def finish(b):
                for j in range(3):
                    mask_silu(b * HEADS + 7, 7, j)

            batches(pool, program)
            finish(BATCH - 1)

        @block.tensor
        def _(pe):
            def into_x(part, b, key, signal=None, count=None):
                bank, _ = x_use(part, b, key)
                at = b if isinstance(b, int) else 1
                before = X_PLAN[part][0][key][2]
                if before:
                    old, back = before
                    read = x_read(b, old)[0]
                    if read is not signal:
                        pe.wait_ge(*x_read(b - back, old))
                    elif x_read(at - back, old)[1] > count(at):
                        pe.wait_ge(*x_read(b - back, old))
                        return X[bank], x_filled[bank]
                if signal is not None:
                    pe.wait_ge(signal, count(b))
                return X[bank], x_filled[bank]

            def transpose_x(part, b, s, nb):
                pe.wait_ge(ln.done, nb)
                for k in range(KD):
                    bank, filled = into_x(part, b, ("XT", s, k))
                    for n in range(TT):
                        last = pe.transpose(bank[:, n * P:(n + 1) * P], xb[:, n, k * P:(k + 1) * P], ident[:, :])
                    last.then_inc(filled, 1)

            def project(part, b, s, t, p):
                bank, filled = into_x(part, b, ("proj", s, t))
                cols = slice(t * INNER + p * P, t * INNER + (p + 1) * P)
                n = 0
                for k in range(KD):
                    for a, c in PRODUCTS:
                        last = pe.matmul(bank[:, :], sh.W[:, a, k, cols], xT[:, c, k, :],
                                         start=(n == 0), stop=(n == 3 * KD - 1))
                        n += 1
                last.then_inc(filled, 1)

            def values(part, b, s):
                bank, filled = into_x(part, b, ("V", s, 0))
                half, two = v_piece(s)
                cols = slice(VC * INNER + half * 2 * P, VC * INNER + (half + 1) * 2 * P)
                for i in range(2):
                    tok = slice((2 * two + i) * P, (2 * two + i + 1) * P)
                    m = 0
                    for k in range(KD):
                        for a, c in PRODUCTS:
                            last = pe.matmul(bank[:, i * 256:(i + 1) * 256], xT[:, a, k, tok], sh.W[:, c, k, cols],
                                             start=(m == 0), stop=(m == 3 * KD - 1))
                            m += 1
                last.then_inc(filled, 1)

            def turn_weights(part, b, s, groups):
                for n in groups:
                    bank, filled = into_x(part, b, ("W", s, n))
                    which, blocks, _ = weight_group(n)
                    if which < 3:
                        pe.wait_ge(made_float, which + 1)
                    else:
                        pe.wait_ge(w_loaded[3], 16)
                    for i, source in enumerate(blocks):
                        last = pe.transpose(bank[:, i * P:(i + 1) * P], source, ident[:, :])
                    last.then_inc(filled, 1)

            def look_ahead(part, b, s, j):
                if s % 2 == 0 and j == 0:
                    pe.wait_ge(qu_twice, (b * PAIRS + s // 2 + 1) * 32)
                    bank, filled = into_x(part, b, ("L", s, j), proj_low,
                                          lambda b: proj_count(b * PAIRS + s // 2, KU))
                else:
                    bank, filled = into_x(part, b, ("L", s, j))
                for w in ROWS[j]:
                    J, at = w - 1, WIDE[w] - GROUP[j][0]
                    for a in (HIGH, LOW):
                        last = pe.matmul(bank[:, at:at + w * P], ku_s[:, s % 2, J * P:(J + 1) * P],
                                         qu_s[:, s % 2, a, 0:w * P], start=(a == 0), stop=(a == 1))
                last.then_inc(filled, 1)

            def term1(part, b, s, j):
                par = (s // 2) % 2
                if s % 2 == 0 and j == 0:
                    pe.wait_ge(qc_twice, (b * PAIRS + s // 2 + 1) * 32)
                    bank, filled = into_x(part, b, ("T", s, j), proj_low,
                                          lambda b: proj_count(b * PAIRS + s // 2, VU))
                else:
                    bank, filled = into_x(part, b, ("T", s, j))
                for w in ROWS[j]:
                    J, at = TT - w, WIDE[w] - GROUP[j][0]
                    for a in (HIGH, LOW):
                        last = pe.matmul(bank[:, at:at + w * P], vu_s[:, s % 2, J * P:(J + 1) * P],
                                         qc_s[:, par, s % 2, a, J * P:SEQ], start=(a == 0), stop=(a == 1))
                last.then_inc(filled, 1)

            def scores(g, s, j):
                hp, par, slot = s % 2, (s // 2) % 2, (s + j) % 2
                if not (isinstance(g, int) and 3 * g + j < 2):
                    pe.wait_ge(scores_emptied, 3 * g + j - 1)
                for w in ROWS[j]:
                    I, at = w - 1, WIDE[w] - GROUP[j][0]
                    for a in (HIGH, LOW):
                        pe.matmul(Sc[slot][:, at:at + w * P], qc_s[:, par, hp, a, I * P:(I + 1) * P],
                                  kc_s[:, par, hp, 0:w * P], start=(a == 0), stop=(a == 1))
                if j == 0:
                    pe.wait_ge(T_ready, after(g, 3, 2))
                    pe.wait_ge(L_ready, after(g, 3, 2))
                for w in ROWS[j]:
                    I, at = w - 1, WIDE[w] - GROUP[j][0]
                    for J in range(I, -1, -1):
                        to = WIDE[TT - J] + (I - J) * P
                        for n, (a, c) in enumerate(PRODUCTS):
                            last = pe.matmul(Su[slot][:, at:at + (J + 1) * P], T_s[:, hp, a, to:to + P],
                                             L_s[:, hp, c, WIDE[J + 1]:WIDE[J + 1] + (J + 1) * P],
                                             start=(J == I and n == 0), stop=(J == 0 and n == 2))
                last.then_inc(scores_filled, 1)

            def turn_probs(part, b, s, g, j):
                hp = s % 2
                if j == 0:
                    pe.wait_ge(prob_ready, after(g, 3, 2))
                bank, filled = into_x(part, b, ("PT", s, j))
                for w in ROWS[j]:
                    K, at = TT - w, WIDE[w] - GROUP[j][0]
                    for I in range(K, TT):
                        last = pe.transpose(bank[:, at + (I - K) * P:at + (I - K + 1) * P],
                                            prob[:, hp, WIDE[I + 1] + K * P:WIDE[I + 1] + (K + 1) * P],
                                            ident[:, :])
                last.then_inc(filled, 1)

            def attend(part, b, s, g):
                slot = (s - 2) % HEADS
                if (s - 2) % 4 == 0:
                    pe.wait_ge(v_low, v_count(b, s - 2))
                bank, filled = into_x(part, b, ("O", s, 0), PT_low,
                                      lambda b: after(b * HEADS + s - 2, 3, 2))
                for K in range(TT):
                    at = WIDE[TT - K]
                    for c in (HIGH, LOW):
                        last = pe.matmul(bank[:, K * P:SEQ], v_s[:, slot // 4, K, slot % 4, :, :],
                                         PT_s[:, c, at:at + (TT - K) * P],
                                         start=(K == 0 and c == HIGH), stop=(K == TT - 1 and c == LOW))
                last.then_inc(filled, 1)

            def even_step(part, b, s, g, s1, back1, back2, ahead):
                if back1:
                    scores(g - 1, s1, 0)
                look_ahead(part, b, s, 0)
                look_ahead(part, b, s, 1)
                if back2:
                    turn_probs(part, b, s, g - 2, 0)
                    turn_probs(part, b, s, g - 2, 1)
                    turn_probs(part, b, s, g - 2, 2)
                look_ahead(part, b, s, 2)
                if back1:
                    scores(g - 1, s1, 1)
                term1(part, b, s, 0)
                if s == 6:
                    transpose_x(part, b, s, b + 1)
                if back2:
                    attend(part, b, s, g - 2)
                if back1:
                    scores(g - 1, s1, 2)
                term1(part, b, s, 1)
                term1(part, b, s, 2)
                if ahead:
                    if s == 6:
                        pe.wait_ge(xT_low, (b + 1) * KD)
                    project(part, b, s, QC, (s // 2 + 1) % PAIRS)
                    values(part, b, s)
                    project(part, b, s, KC, (s // 2 + 1) % PAIRS)
                if part == LAST:
                    turn_weights(part, b, s, WEIGHTS_IN_STEP.get(s, ()))

            def odd_step(part, b, s, g, s1, back1, back2, ahead):
                look_ahead(part, b, s, 0)
                if back1:
                    scores(g - 1, s1, 0)
                look_ahead(part, b, s, 1)
                if back2:
                    turn_probs(part, b, s, g - 2, 0)
                look_ahead(part, b, s, 2)
                if ahead:
                    project(part, b, s, QU, (s // 2 + 1) % PAIRS)
                if back2:
                    turn_probs(part, b, s, g - 2, 1)
                if back1:
                    scores(g - 1, s1, 1)
                term1(part, b, s, 0)
                if back2:
                    turn_probs(part, b, s, g - 2, 2)
                term1(part, b, s, 1)
                if back1:
                    scores(g - 1, s1, 2)
                if back2:
                    attend(part, b, s, g - 2)
                term1(part, b, s, 2)
                if ahead:
                    project(part, b, s, KU, (s // 2 + 1) % PAIRS)
                    project(part, b, s, VU, (s // 2 + 1) % PAIRS)
                if part == LAST:
                    turn_weights(part, b, s, WEIGHTS_IN_STEP.get(s, ()))

            def program(b, part):
                run_steps(b, part, even_step, odd_step)

            def finish(b):
                g = b * HEADS + HEADS
                scores(g - 1, 7, 0)
                turn_weights(LAST, b, HEADS, (6, 7))
                for j in range(3):
                    turn_probs(LAST, b, HEADS, g - 2, j)
                scores(g - 1, 7, 1)
                attend(LAST, b, HEADS, g - 2)
                scores(g - 1, 7, 2)
                turn_weights(LAST, b, HEADS, range(8, 11))
                for j in range(3):
                    turn_probs(LAST, b, HEADS + 1, g - 1, j)
                turn_weights(LAST, b, HEADS, (11, 12))
                attend(LAST, b, HEADS + 1, g - 1)

            for t in FIRST_PAIR:
                project(FIRST, 0, -2, t, 0)
            values(FIRST, 0, -2)
            batches(pe, program)
            finish(BATCH - 1)

        @block.scalar
        def _(act):
            def from_x(part, b, key):
                bank, nth = x_use(part, b, key)
                act.wait_ge(x_filled[bank], nth)
                return X[bank]

            def high_xT(part, b, s):
                for k in range(KD):
                    bank = from_x(part, b, ("XT", s, k))
                    act.activation(xT[:, HIGH, k, :], bank[:, :], ACT.Copy).then_inc(xT_high, 1)

            def high_proj(part, b, s, t, par):
                bank = from_x(part, b, ("proj", s, t))
                for h in range(2):
                    rows = slice(h * DH, (h + 1) * DH)
                    dst = {KU: ku_s[rows, h, :], VU: vu_s[rows, h, :], KC: kc_s[rows, par, h, :],
                           QU: qu_s[rows, h, HIGH, :], QC: qc_s[rows, par, h, HIGH, :]}[t]
                    last = act.activation(dst, bank[rows, :], ACT.Copy)
                last.then_inc(proj_high, 1)

            def high_values(part, b, s):
                bank = from_x(part, b, ("V", s, 0))
                half, two = v_piece(s)
                act.activation(v_s[:, half, 2 * two:2 * two + 2, :, HIGH, :],
                               bank[:, :].rearrange("p (n h c) -> p n h c", n=2, h=4), ACT.Copy).then_inc(v_high, 1)

            def high_weights(part, b, s, groups):
                for n in groups:
                    bank = from_x(part, b, ("W", s, n))
                    _, blocks, (high, _) = weight_group(n)
                    act.activation(high, shaped(bank, blocks, high), ACT.Copy).then_inc(w_high, 1)

            def tanh_of_L(part, b, s, g, j):
                bank = from_x(part, b, ("L", s, j))
                c, n = GROUP[j]
                if not (isinstance(g, int) and g == 0):
                    act.wait_ge(L_ready, after(g - 1, 3, j))
                act.activation(tanh_l[:, c:c + n], bank[:, 0:n], ACT.Tanh, scale=LOOK_SCALE).then_inc(tanh_done, 1)

            def high_T(part, b, s, g, j):
                bank = from_x(part, b, ("T", s, j))
                c, n = GROUP[j]
                if not (isinstance(g, int) and g < 2):
                    act.wait_ge(scores_filled, after(g - 2, 3, 2))
                act.activation(T_s[:, s % 2, HIGH, c:c + n], bank[:, 0:n], ACT.Copy).then_inc(T_high, 1)

            def high_L(g, s, j):
                c, n = GROUP[j]
                act.wait_ge(tanh_masked, after(g, 3, j))
                if not (isinstance(g, int) and g < 2):
                    act.wait_ge(scores_filled, after(g - 2, 3, 2))
                act.activation(L_s[:, s % 2, HIGH, c:c + n], tanh_l[:, c:c + n], ACT.Copy, bias=1.0) \
                   .then_inc(L_high, 1)

            def gate_of(g, s, j):
                c, n = GROUP[j]
                if not (isinstance(g, int) and g == 0):
                    act.wait_ge(scores_emptied, after(g - 1, 3, j))
                act.wait_ge(scores_filled, after(g, 3, j))
                act.activation(gate[:, c:c + n], Su[(s + j) % 2][:, 0:n], ACT.Tanh, scale=SU_SCALE) \
                   .then_inc(gate_done, 1)

            def exp_of(g, s, j):
                hp = s % 2
                act.wait_ge(scores_emptied, after(g, 3, j))
                for w in ROWS[j]:
                    v = prob[:, hp, WIDE[w]:WIDE[w] + w * P]
                    last = act.activation(v, v, ACT.Exp, bias=least[:, hp, w - 1:w], scale=-1.0,
                                          accum_out=total[:, hp, w - 1:w])
                last.then_inc(exp_done, 1)

            def high_PT(part, b, s, g, j):
                bank = from_x(part, b, ("PT", s, j))
                c, n = GROUP[j]
                act.activation(PT_s[:, HIGH, c:c + n], bank[:, 0:n], ACT.Copy).then_inc(PT_high, 1)

            def copy_o_low(part, b, s, g):
                bank = from_x(part, b, ("O", s, 0))
                if not (isinstance(g, int) and g == 0):
                    act.wait_ge(o_copied, g)
                act.activation(o_low[:, :], bank[DH:P, :], ACT.Copy).then_inc(o_low_copied, 1)

            def even_step(part, b, s, g, s1, back1, back2, ahead):
                par = (s // 2 + 1) % 2
                if back1:
                    gate_of(g - 1, s1, 0)
                tanh_of_L(part, b, s, g, 0)
                tanh_of_L(part, b, s, g, 1)
                if back2:
                    high_PT(part, b, s, g - 2, 0)
                    high_PT(part, b, s, g - 2, 1)
                tanh_of_L(part, b, s, g, 2)
                if back2:
                    high_PT(part, b, s, g - 2, 2)
                high_L(g, s, 0)
                if back1:
                    gate_of(g - 1, s1, 1)
                high_T(part, b, s, g, 0)
                if s == 6:
                    high_xT(part, b, s)
                if back1:
                    exp_of(g - 1, s1, 0)
                if back2:
                    copy_o_low(part, b, s, g - 2)
                high_L(g, s, 1)
                if back1:
                    gate_of(g - 1, s1, 2)
                high_T(part, b, s, g, 1)
                high_T(part, b, s, g, 2)
                if back1:
                    exp_of(g - 1, s1, 1)
                high_L(g, s, 2)
                if ahead:
                    high_proj(part, b, s, QC, par)
                    high_values(part, b, s)
                if back1:
                    exp_of(g - 1, s1, 2)
                if ahead:
                    high_proj(part, b, s, KC, par)
                if part == LAST:
                    high_weights(part, b, s, WEIGHTS_IN_STEP.get(s, ()))

            def odd_step(part, b, s, g, s1, back1, back2, ahead):
                par = (s // 2 + 1) % 2
                tanh_of_L(part, b, s, g, 0)
                if back1:
                    gate_of(g - 1, s1, 0)
                tanh_of_L(part, b, s, g, 1)
                if back2:
                    high_PT(part, b, s, g - 2, 0)
                high_L(g, s, 0)
                high_L(g, s, 1)
                if ahead:
                    high_proj(part, b, s, QU, par)
                if back2:
                    high_PT(part, b, s, g - 2, 1)
                tanh_of_L(part, b, s, g, 2)
                if back1:
                    exp_of(g - 1, s1, 0)
                    gate_of(g - 1, s1, 1)
                if back2:
                    high_PT(part, b, s, g - 2, 2)
                high_T(part, b, s, g, 0)
                high_L(g, s, 2)
                high_T(part, b, s, g, 1)
                if back1:
                    gate_of(g - 1, s1, 2)
                high_T(part, b, s, g, 2)
                if back1:
                    exp_of(g - 1, s1, 1)
                if ahead:
                    high_proj(part, b, s, KU, par)
                if back2:
                    copy_o_low(part, b, s, g - 2)
                if back1:
                    exp_of(g - 1, s1, 2)
                if ahead:
                    high_proj(part, b, s, VU, par)
                if part == LAST:
                    high_weights(part, b, s, WEIGHTS_IN_STEP.get(s, ()))

            def program(b, part):
                run_steps(b, part, even_step, odd_step)

            def finish(b):
                g = b * HEADS + HEADS
                gate_of(g - 1, 7, 0)
                high_weights(LAST, b, HEADS, (6, 7))
                for j in range(3):
                    high_PT(LAST, b, HEADS, g - 2, j)
                gate_of(g - 1, 7, 1)
                exp_of(g - 1, 7, 0)
                copy_o_low(LAST, b, HEADS, g - 2)
                gate_of(g - 1, 7, 2)
                exp_of(g - 1, 7, 1)
                exp_of(g - 1, 7, 2)
                high_weights(LAST, b, HEADS, range(8, 11))
                for j in range(3):
                    high_PT(LAST, b, HEADS + 1, g - 1, j)
                high_weights(LAST, b, HEADS, (11, 12))
                copy_o_low(LAST, b, HEADS + 1, g - 1)

            for t in FIRST_PAIR:
                high_proj(FIRST, 0, -2, t, 0)
            high_values(FIRST, 0, -2)
            batches(act, program)
            finish(BATCH - 1)

        @block.vector
        def _(dve):
            def x_bank(part, key):
                return X[X_PLAN[part][0][key][0]]

            def low_xT(part, b, s, nb):
                for k in range(KD):
                    bank = x_bank(part, ("XT", s, k))
                    dve.wait_ge(xT_high, (nb - 1) * KD + k + 1)
                    dve.tensor_tensor(xT[:, LOW, k, :], bank[:, :], xT[:, HIGH, k, :].bitcast(F32), ALU.subtract) \
                       .then_inc(xT_low, 1)

            def low_proj(part, b, s, t, par, q):
                bank = x_bank(part, ("proj", s, t))
                dve.wait_ge(proj_high, proj_count(q, t))
                for h in range(2):
                    rows, other = slice(h * DH, (h + 1) * DH), slice((1 - h) * DH, (2 - h) * DH)
                    high, out = {KU: (ku_s[rows, h, :], ku_s[other, h, :]),
                                 VU: (vu_s[rows, h, :], vu_s[other, h, :]),
                                 KC: (kc_s[rows, par, h, :], kc_s[other, par, h, :]),
                                 QU: (qu_s[rows, h, HIGH, :], qu_s[rows, h, LOW, :]),
                                 QC: (qc_s[rows, par, h, HIGH, :], qc_s[rows, par, h, LOW, :])}[t]
                    last = dve.tensor_tensor(out, bank[rows, :], high.bitcast(F32), ALU.subtract)
                last.then_inc(proj_low, 1)

            def low_values(part, b, s):
                bank = x_bank(part, ("V", s, 0))
                half, two = v_piece(s)
                dve.wait_ge(v_high, v_count(b, s))
                dve.tensor_tensor(v_s[:, half, 2 * two:2 * two + 2, :, LOW, :],
                                  bank[:, :].rearrange("p (n h c) -> p n h c", n=2, h=4),
                                  v_s[:, half, 2 * two:2 * two + 2, :, HIGH, :].bitcast(F32), ALU.subtract) \
                   .then_inc(v_low, 1)

            def make_float(n):
                dve.wait_ge(w_loaded[n], 16)
                ints = (int_gate[:, :, :], int_up[:, :, :], int_down)[n]
                dve.tensor_copy(natural[n], ints).then_inc(made_float, 1)

            def low_weights(part, b, s, groups):
                for n in groups:
                    bank = x_bank(part, ("W", s, n))
                    _, blocks, (high, low) = weight_group(n)
                    dve.wait_ge(w_high, n + 1)
                    dve.tensor_tensor(low, shaped(bank, blocks, low), high.bitcast(F32), ALU.subtract) \
                       .then_inc(w_low, 1)

            def take_low_max(n, groups):
                dve.wait_ge(w_low, groups)
                low = (sh.gate_w, sh.up_w, sh.down_w)[n][:, LOW]
                dve.tensor_reduce(low_max[:, n:n + 1], low.bitcast(F32), mybir.AxisListType.XY, ALU.max,
                                  apply_absolute_value=True).then_inc(low_max_taken, 1)

            def take_has_low():
                dve.wait_ge(low_max_gathered, 16)
                dve.tensor_reduce(largest[:, :], low_row[:, :], mybir.AxisListType.X, ALU.max).then_inc(largest_taken, 1)
                dve.wait_ge(largest_taken, 1)
                dve.tensor_scalar(sh.has_low[:, :], largest[:, :], 0.0, None, ALU.is_gt)

            def low_L(g, s, j):
                c, n = GROUP[j]
                dve.wait_ge(L_high, after(g, 3, j))
                dve.scalar_tensor_tensor(L_s[:, s % 2, LOW, c:c + n], tanh_l[:, c:c + n], 1.0,
                                         L_s[:, s % 2, HIGH, c:c + n].bitcast(F32), ALU.add, ALU.subtract) \
                   .then_inc(L_ready, 1)

            def low_T(part, b, s, g, j):
                bank = x_bank(part, ("T", s, j))
                c, n = GROUP[j]
                dve.wait_ge(T_high, after(g, 3, j))
                dve.tensor_tensor(T_s[:, s % 2, LOW, c:c + n], bank[:, 0:n],
                                  T_s[:, s % 2, HIGH, c:c + n].bitcast(F32), ALU.subtract) \
                   .then_inc(T_low, 1)

            def silu_of(g, s, j):
                c, n = GROUP[j]
                dve.wait_ge(gate_done, after(g, 3, j))
                dve.scalar_tensor_tensor(gate[:, c:c + n], gate[:, c:c + n], 1.0, Su[(s + j) % 2][:, 0:n],
                                         ALU.add, ALU.mult).then_inc(silu_done, 1)

            def minus_scores(g, s, j):
                hp = s % 2
                wait_before(dve, silu_masked, after(g, 3, j))
                if j == 0 and not (isinstance(g, int) and g < 2):
                    wait_before(dve, PT_high, after(g - 2, 3, 2))
                for w in ROWS[j]:
                    at = WIDE[w] - GROUP[j][0]
                    last = dve.tensor_tensor_reduce(prob[:, hp, WIDE[w]:WIDE[w] + w * P],
                                                    Sc[(s + j) % 2][:, at:at + w * P],
                                                    gate[:, WIDE[w]:WIDE[w] + w * P], SU_SCALE, NO_SCORE,
                                                    ALU.add, ALU.min, least[:, hp, w - 1:w])
                last.then_inc(scores_emptied, 1)

            def inverse(g, s, j):
                hp = s % 2
                for i, w in enumerate(ROWS[j]):
                    if i == 0:
                        dve.wait_ge(exp_done, after(g, 3, j))
                    last = dve.reciprocal(inv[:, hp, w - 1:w], total[:, hp, w - 1:w])
                last.then_inc(inv_done, 1)

            def low_PT(part, b, s, g, j):
                bank = x_bank(part, ("PT", s, j))
                c, n = GROUP[j]
                dve.wait_ge(PT_high, after(g, 3, j))
                dve.tensor_tensor(PT_s[:, LOW, c:c + n], bank[:, 0:n],
                                  PT_s[:, HIGH, c:c + n].bitcast(F32), ALU.subtract) \
                   .then_inc(PT_low, 1)

            def sum_o(part, b, s, g):
                slot = (s - 2) % HEADS
                rows, par = slice((slot % 2) * DH, (slot % 2 + 1) * DH), (slot // 2) % 2
                if slot % 2 == 0 and not (isinstance(b, int) and b * PAIRS + (s - 2) // 2 < 2):
                    dve.wait_ge(o_stored[par], ((b * PAIRS + (s - 2) // 2 - par) // 2) * 16
                                if isinstance(b, int) else (b * (PAIRS // 2) + ((s - 2) // 2 - par) // 2) * 16)
                dve.wait_ge(o_low_copied, g + 1)
                dve.tensor_tensor(o_s[rows, par, :], x_bank(part, ("O", s, 0))[0:DH, :], o_low[:, :], ALU.add) \
                   .then_inc(o_copied, 1)

            def even_step(part, b, s, g, s1, back1, back2, ahead):
                par, q = (s // 2 + 1) % 2, b * PAIRS + s // 2 + 1
                if back1:
                    silu_of(g - 1, s1, 0)
                if back2:
                    low_PT(part, b, s, g - 2, 0)
                    low_PT(part, b, s, g - 2, 1)
                    low_PT(part, b, s, g - 2, 2)
                if back1:
                    minus_scores(g - 1, s1, 0)
                low_L(g, s, 0)
                if back1:
                    silu_of(g - 1, s1, 1)
                low_T(part, b, s, g, 0)
                if s == 6:
                    low_xT(part, b, s, b + 1)
                if back1:
                    inverse(g - 1, s1, 0)
                if back2:
                    sum_o(part, b, s, g - 2)
                if back1:
                    minus_scores(g - 1, s1, 1)
                    silu_of(g - 1, s1, 2)
                low_T(part, b, s, g, 1)
                low_L(g, s, 1)
                low_T(part, b, s, g, 2)
                if back1:
                    inverse(g - 1, s1, 1)
                    minus_scores(g - 1, s1, 2)
                low_L(g, s, 2)
                if ahead:
                    low_proj(part, b, s, QC, par, q)
                if back1:
                    inverse(g - 1, s1, 2)
                if ahead:
                    low_values(part, b, s)
                    low_proj(part, b, s, KC, par, q)
                if part == LAST:
                    if s == 6:
                        make_float(1)
                    low_weights(part, b, s, WEIGHTS_IN_STEP.get(s, ()))

            def odd_step(part, b, s, g, s1, back1, back2, ahead):
                par, q = (s // 2 + 1) % 2, b * PAIRS + s // 2 + 1
                if part == LAST and s == 7:
                    take_low_max(0, 4)
                if s == 5:
                    ln.scale(dve, b + 1)
                if s == 3:
                    ln.take_stats(dve, b + 1)
                if back1:
                    silu_of(g - 1, s1, 0)
                if back2:
                    low_PT(part, b, s, g - 2, 0)
                low_L(g, s, 0)
                if back1:
                    minus_scores(g - 1, s1, 0)
                if ahead:
                    low_proj(part, b, s, QU, par, q)
                if back2:
                    low_PT(part, b, s, g - 2, 1)
                if back1:
                    silu_of(g - 1, s1, 1)
                    inverse(g - 1, s1, 0)
                if back2:
                    low_PT(part, b, s, g - 2, 2)
                low_T(part, b, s, g, 0)
                if back1:
                    minus_scores(g - 1, s1, 1)
                    silu_of(g - 1, s1, 2)
                low_T(part, b, s, g, 1)
                low_T(part, b, s, g, 2)
                low_L(g, s, 1)
                if back1:
                    inverse(g - 1, s1, 1)
                low_L(g, s, 2)
                if back1:
                    minus_scores(g - 1, s1, 2)
                if ahead:
                    low_proj(part, b, s, KU, par, q)
                if back1:
                    inverse(g - 1, s1, 2)
                if back2:
                    sum_o(part, b, s, g - 2)
                if ahead:
                    low_proj(part, b, s, VU, par, q)
                if part == LAST:
                    if s == 5:
                        make_float(0)
                    low_weights(part, b, s, WEIGHTS_IN_STEP.get(s, ()))

            def program(b, part):
                run_steps(b, part, even_step, odd_step)

            def norm(g, s, j):
                wait_before(dve, inv_done, after(g, 3, j))
                for w in ROWS[j]:
                    v = prob[:, s % 2, WIDE[w]:WIDE[w] + w * P]
                    last = dve.tensor_scalar(v, v, inv[:, s % 2, w - 1:w], None, ALU.mult)
                last.then_inc(prob_ready, 1)

            def finish(b):
                g = b * HEADS + HEADS
                make_float(2)
                silu_of(g - 1, 7, 0)
                low_weights(LAST, b, HEADS, (6, 7))
                minus_scores(g - 1, 7, 0)
                for j in range(3):
                    low_PT(LAST, b, HEADS, g - 2, j)
                take_low_max(1, 8)
                silu_of(g - 1, 7, 1)
                inverse(g - 1, 7, 0)
                minus_scores(g - 1, 7, 1)
                norm(g - 1, 7, 0)
                silu_of(g - 1, 7, 2)
                sum_o(LAST, b, HEADS, g - 2)
                inverse(g - 1, 7, 1)
                minus_scores(g - 1, 7, 2)
                norm(g - 1, 7, 1)
                inverse(g - 1, 7, 2)
                norm(g - 1, 7, 2)
                low_weights(LAST, b, HEADS, range(8, 11))
                for j in range(3):
                    low_PT(LAST, b, HEADS + 1, g - 1, j)
                take_low_max(2, 11)
                low_weights(LAST, b, HEADS, (11, 12))
                sum_o(LAST, b, HEADS + 1, g - 1)
                take_has_low()

            for t in FIRST_PAIR:
                low_proj(FIRST, 0, -2, t, 0, 0)
            low_values(FIRST, 0, -2)
            batches(dve, program)
            finish(BATCH - 1)


def ffn_and_sum(nc, x, sh, heads_out, out):
    ctx = ExitStack()
    with ctx:
        def sb(name, shape, dt):
            return ctx.enter_context(nc.sbuf_tensor(name, shape, dt))

        def sem(name):
            return ctx.enter_context(nc.semaphore(name))

        xb, xT = sh.xb, sh.xT
        xres = sb("f_xres", [P, TT, DIM], F32)
        act_s = sb("f_act", [P, 2, SEQ], F32)
        h_s = sb("f_h", [P, 2, HT, SEQ], F32R)
        o_in = sb("f_o_in", [P, OT, SEQ], F32)
        o_s = sb("f_o", [P, 2, OT, SEQ], F32R)
        y_s = sb("f_y", [P, TT, DIM], F32)

        def pb(name):
            return ctx.enter_context(nc.psum_tensor(name, [P, 512], F32))

        G = [pb(f"f_G{i}") for i in range(2)]
        U = [pb(f"f_U{i}") for i in range(2)]
        Y = [pb(f"f_Y{i}") for i in range(2)]
        XT = [pb(f"f_XT{i}") for i in range(2)]

        xres_loaded = sem("f_xres_loaded")
        o_loaded = sem("f_o_loaded")
        xT_filled = sem("f_xT_filled")
        xT_high = sem("f_xT_high")
        xT_low = sem("f_xT_low")
        gu_filled = sem("f_gu_filled")
        tanh_done = sem("f_tanh_done")
        gated = sem("f_gated")
        hidden_done = sem("f_hidden_done")
        h_high = sem("f_h_high")
        h_low = sem("f_h_low")
        o_high = sem("f_o_high")
        o_low = sem("f_o_low")
        o_used = sem("f_o_used")
        y_filled = sem("f_y_filled")
        y_done = sem("f_y_done")
        y_stored = sem("f_y_stored")
        ticks = sem("f_ticks")
        norm = LayerNorm(nc, ctx, "f", sh, 1, ticks)

        block = ctx.enter_context(nc.Block())

        def batches(eng, program):
            program(0, FIRST)
            with eng.Fori(1, BATCH - 1) as b:
                program(b, MIDDLE)
            program(BATCH - 1, LAST)

        @block.sync
        def _(sp):
            def rows(t, b, n):
                return t[bass.ds(b * n, n), :]

            def store_y(b):
                sp.wait_ge(y_done, 2 * b + 2)
                sp.sem_inc(ticks, 1)
                sp.dma_start(rows(out, b, SEQ).rearrange("(n p) d -> p n d", p=P), y_s[:, :, :]).then_inc(y_stored, 16)

            def load_o(b):
                sp.dma_start(o_in[:, :, :], rows(heads_out, b, INNER).rearrange("(n p) d -> p n d", p=P)).then_inc(o_loaded, 16)

            def program(b, part):
                if part == FIRST:
                    load_o(0)
                if part != LAST:
                    if part != FIRST:
                        sp.wait_ge(xT_low, b * KD)
                        sp.sem_inc(ticks, 1)
                    norm.load(sp, x, b + 1)
                if part == FIRST:
                    for stored in sh.o_stored:
                        sp.wait_ge(stored, 16 * BATCH * PAIRS // 2)
                if part != FIRST:
                    store_y(b - 1)
                sp.dma_start(xres[:, :, :], rows(x, b, SEQ).rearrange("(n p) d -> p n d", p=P)).then_inc(xres_loaded, 16)
                if part != LAST:
                    sp.wait_ge(o_low, OT * (b + 1))
                    sp.sem_inc(ticks, 1)
                    load_o(b + 1)

            batches(sp, program)
            store_y(BATCH - 1)
            sp.wait_ge(y_stored, 16 * BATCH)

        @block.gpsimd
        def _(pool):
            def program(b, part):
                if part != LAST:
                    norm.take_rstd(pool, b + 1)

            batches(pool, program)

        @block.tensor
        def _(pe):
            def transpose_x(b):
                pe.wait_ge(norm.done, b)
                if not (isinstance(b, int) and b == 1):
                    pe.wait_ge(xT_low, (b - 1) * KD)
                for k in range(KD):
                    for n in range(TT):
                        last = pe.transpose(XT[k][:, n * P:(n + 1) * P], xb[:, n, k * P:(k + 1) * P], sh.ident[:, :])
                    last.then_inc(xT_filled, 1)

            def gate_up(b, m, products):
                if not (isinstance(b, int) and b * HT + m < 2):
                    pe.wait_ge(hidden_done, b * HT + m - 1)
                for bank, w in ((G[m % 2], sh.gate_w), (U[m % 2], sh.up_w)):
                    n = 0
                    for k in range(KD):
                        for a, c in products:
                            last = pe.matmul(bank[:, :], w[:, a, k, m * P:(m + 1) * P], xT[:, c, k, :],
                                             start=(n == 0), stop=(n == len(products) * KD - 1))
                            n += 1
                last.then_inc(gu_filled, 1)

            def into_y(parts, w, m, begin, end, products):
                for t in range(TT):
                    for n, (c, a) in enumerate(products):
                        last = pe.matmul(Y[t // 2][:, (t % 2) * DIM:(t % 2 + 1) * DIM],
                                         parts[:, a, m, t * P:(t + 1) * P], w[:, c, m, :],
                                         start=(begin and n == 0 and t % 2 == 0), stop=(end and n == len(products) - 1),
                                         skip_group_check=True)
                    if end and t % 2 == 1:
                        last.then_inc(y_filled, 1)
                return last

            def down(b, m, products):
                if m == 0 and not (isinstance(b, int) and b == 0):
                    pe.wait_ge(y_done, 2 * b)
                pe.wait_ge(h_low, b * HT + m + 1)
                into_y(h_s, sh.down_w, m, m == 0, m == HT - 1, products)

            def project_o(b, m):
                pe.wait_ge(o_low, b * OT + m + 1)
                into_y(o_s, sh.out_w, m, False, False, PRODUCTS).then_inc(o_used, 1)

            def program(b, part, products):
                if part != FIRST:
                    pe.wait_ge(xT_low, b * KD)
                gate_up(b, 0, products)
                gate_up(b, 1, products)
                if part != FIRST:
                    down(b - 1, 4, products)
                    down(b - 1, 5, products)
                gate_up(b, 2, products)
                gate_up(b, 3, products)
                down(b, 0, products)
                down(b, 1, products)
                gate_up(b, 4, products)
                project_o(b, 0)
                down(b, 2, products)
                gate_up(b, 5, products)
                if part != LAST:
                    transpose_x(b + 1)
                project_o(b, 1)
                project_o(b, 2)
                down(b, 3, products)
                project_o(b, 3)
                if part == LAST:
                    down(b, 4, products)
                    down(b, 5, products)

            has_low = pe.value_load(sh.has_low[0:1, 0:1], min_val=0, max_val=1)
            with pe.If(has_low == 0):
                batches(pe, lambda b, part: program(b, part, PRODUCTS[0:2]))
            with pe.Else():
                batches(pe, lambda b, part: program(b, part, PRODUCTS))

        @block.scalar
        def _(act):
            def high_xT(b):
                for k in range(KD):
                    act.wait_ge(xT_filled, (b - 1) * KD + k + 1)
                    act.activation(xT[:, HIGH, k, :], XT[k][:, :], ACT.Copy).then_inc(xT_high, 1)

            def tanh_of(b, m):
                act.wait_ge(gu_filled, b * HT + m + 1)
                if not (isinstance(b, int) and b * HT + m < 2):
                    act.wait_ge(h_low, b * HT + m - 1)
                act.activation(act_s[:, m % 2, :], G[m % 2][:, :], ACT.Tanh, scale=0.5 * INT_SCALE).then_inc(tanh_done, 1)

            def high_h(b, m):
                act.wait_ge(hidden_done, b * HT + m + 1)
                act.activation(h_s[:, HIGH, m, :], act_s[:, m % 2, :], ACT.Copy, scale=HIDDEN_SCALE).then_inc(h_high, 1)

            def high_o(b, m):
                act.wait_ge(o_loaded, b * 16 + 16)
                if not (isinstance(b, int) and b == 0):
                    act.wait_ge(o_used, b * OT + m + 1 - OT)
                act.activation(o_s[:, HIGH, m, :], o_in[:, m, :], ACT.Copy).then_inc(o_high, 1)

            def program(b, part):
                if part != FIRST:
                    high_h(b - 1, 5)
                tanh_of(b, 0)
                tanh_of(b, 1)
                high_h(b, 0)
                high_o(b, 0)
                high_o(b, 1)
                high_h(b, 1)
                tanh_of(b, 2)
                high_h(b, 2)
                tanh_of(b, 3)
                high_o(b, 2)
                tanh_of(b, 4)
                high_h(b, 3)
                tanh_of(b, 5)
                if part != LAST:
                    high_xT(b + 1)
                high_o(b, 3)
                high_h(b, 4)
                if part == LAST:
                    high_h(b, 5)

            batches(act, program)

        @block.vector
        def _(dve):
            def low_xT(b):
                for k in range(KD):
                    dve.wait_ge(xT_high, (b - 1) * KD + k + 1)
                    dve.tensor_tensor(xT[:, LOW, k, :], XT[k][:, :], xT[:, HIGH, k, :].bitcast(F32), ALU.subtract) \
                       .then_inc(xT_low, 1)

            def gated_of(b, m):
                a = act_s[:, m % 2, :]
                dve.wait_ge(tanh_done, b * HT + m + 1)
                dve.scalar_tensor_tensor(a, a, 1.0, G[m % 2][:, :], ALU.add, ALU.mult).then_inc(gated, 1)

            def hidden(b, m):
                a = act_s[:, m % 2, :]
                dve.wait_ge(gated, b * HT + m + 1)
                dve.tensor_tensor(a, a, U[m % 2][:, :], ALU.mult).then_inc(hidden_done, 1)

            def low_h(b, m):
                dve.wait_ge(h_high, b * HT + m + 1)
                dve.scalar_tensor_tensor(h_s[:, LOW, m, :], act_s[:, m % 2, :], HIDDEN_SCALE,
                                         h_s[:, HIGH, m, :].bitcast(F32), ALU.mult, ALU.subtract).then_inc(h_low, 1)

            def low_o(b, m):
                dve.wait_ge(o_high, b * OT + m + 1)
                dve.tensor_tensor(o_s[:, LOW, m, :], o_in[:, m, :], o_s[:, HIGH, m, :].bitcast(F32),
                                  ALU.subtract).then_inc(o_low, 1)

            def sum_y(b):
                for i in range(2):
                    dve.wait_ge(y_filled, 2 * b + i + 1)
                    if i == 0:
                        dve.wait_ge(xres_loaded, b * 16 + 16)
                        if not (isinstance(b, int) and b == 0):
                            dve.wait_ge(y_stored, b * 16)
                    dve.tensor_tensor(y_s[:, 2 * i:2 * i + 2, :], Y[i][:, :].rearrange("p (n c) -> p n c", n=2),
                                      xres[:, 2 * i:2 * i + 2, :], ALU.add).then_inc(y_done, 1)

            def program(b, part):
                if part != FIRST:
                    low_h(b - 1, 5)
                gated_of(b, 0)
                hidden(b, 0)
                gated_of(b, 1)
                low_h(b, 0)
                hidden(b, 1)
                low_o(b, 0)
                if part != FIRST:
                    sum_y(b - 1)
                low_h(b, 1)
                gated_of(b, 2)
                hidden(b, 2)
                if part != LAST:
                    norm.take_stats(dve, b + 1)
                gated_of(b, 3)
                low_h(b, 2)
                hidden(b, 3)
                if part != LAST:
                    norm.scale(dve, b + 1)
                low_h(b, 3)
                low_o(b, 1)
                gated_of(b, 4)
                hidden(b, 4)
                low_o(b, 2)
                gated_of(b, 5)
                low_o(b, 3)
                if part != LAST:
                    low_xT(b + 1)
                low_h(b, 4)
                hidden(b, 5)
                if part == LAST:
                    low_h(b, 5)
                    sum_y(b)

            batches(dve, program)


def build(nc, x, W_qkv, W_out, w_gate, w_up, w_down, out):
    x_rows = x.rearrange("b n d -> (b n) d")
    out_rows = out.rearrange("b n d -> (b n) d")
    heads_out = nc.dram_tensor("heads_out", [BATCH * INNER, SEQ], F32).ap()
    with ExitStack() as ctx:
        sh = Shared(nc, ctx)
        prologue(nc, x_rows, W_qkv, sh)
        attention(nc, x_rows, w_gate, w_up, w_down, W_out, sh, heads_out)
        ffn_and_sum(nc, x_rows, sh, heads_out, out_rows)


_INS = ["L0_attn_x", "L0_attn_W_qkv", "L0_attn_W_out", "L0_ffn_w_gate", "L0_ffn_w_up", "L0_ffn_w_down"]


def kernel(**inputs):
    import concourse.bacc as bacc
    from concourse.bass_utils import run_bass_kernel_spmd

    nc = bacc.Bacc("TRN2", target_bir_lowering=False, num_devices=1)
    arrays, args = {}, []
    for name in _INS:
        a = np.ascontiguousarray(inputs[name])
        arrays[f"in_{name}"] = a
        args.append(nc.dram_tensor(f"in_{name}", a.shape, mybir.dt.from_np(a.dtype), kind="ExternalInput").ap())
    out = nc.dram_tensor("out", (BATCH, SEQ, DIM), F32, kind="ExternalOutput").ap()
    build(nc, *args, out)
    r = run_bass_kernel_spmd(nc, [arrays], core_ids=[0])
    return r.results[0]["out"]
```
